# Optimizing a Trainium2 kernel written in Bass

```python
import numpy as np
import jax
import jax.numpy as jnp

def _softmax(x, axis=-1):
    return jax.nn.softmax(x, axis=axis)

def _gelu(x):
    return jax.nn.gelu(x, approximate=True)

def _silu(x):
    return jax.nn.silu(x)

def _sigmoid(x):
    return jax.nn.sigmoid(x)

def _layernorm(x, axis=-1, eps=1e-05):
    m = jnp.mean(x, axis=axis, keepdims=True)
    v = jnp.var(x, axis=axis, keepdims=True)
    return (x - m) / jnp.sqrt(v + eps)

def _scatter_add(tgt, idx, src, axis=0):
    return tgt.at[idx].add(src)

def _segment_sum(src, seg, n):
    return jax.ops.segment_sum(src, seg, n)
kernel_name = 'mk_xattn_seq_d4_seqx_r8_4e1169'

def setup_inputs(seed: int=0):
    np.random.seed(seed)
    _w = jnp.asarray

    def _rec_inputs():
        import jax
        import jax.numpy as jnp
        _rk = jax.random.key(seed)
        x = -0.0002928 + 1 * jax.random.normal(jax.random.fold_in(_rk, 1), (2, 256, 128), jnp.float32)
        _lenS = 256 - jax.random.randint(jax.random.fold_in(_rk, 7), (2,), 0, max(1, 256 // 4) + 1, jnp.int32)
        _lenS2 = 512 - jax.random.randint(jax.random.fold_in(_rk, 8), (2,), 0, max(1, 512 // 4) + 1, jnp.int32)
        _ctx_1024P = jax.random.normal(jax.random.fold_in(_rk, 11), (2, 16, 128), jnp.float32)
        _ctx_1024c = jax.random.dirichlet(jax.random.fold_in(_rk, 511), 0.3 * jnp.ones((16,), jnp.float32), (2, 512))
        _ctx_1024t = jnp.einsum('bsk,bkd->bsd', _ctx_1024c, _ctx_1024P)
        _ctx_1024t = _ctx_1024t * jax.lax.rsqrt(jnp.mean(jnp.square(_ctx_1024t)) + 1e-12) * 0.953939
        ctx_1024 = -1.39393e-06 + 0.999914 * (_ctx_1024t + 0.3 * jax.random.normal(jax.random.fold_in(_rk, 611), (2, 512, 128), jnp.float32))
        itok_BxS2_4_31999 = jax.random.randint(jax.random.fold_in(_rk, 12), (2, 512), 4, 4000, jnp.int32)
        _ctxb_2048x64P = jax.random.normal(jax.random.fold_in(_rk, 13), (2, 16, 64), jnp.float32)
        _ctxb_2048x64c = jax.random.dirichlet(jax.random.fold_in(_rk, 513), 0.3 * jnp.ones((16,), jnp.float32), (2, 512))
        _ctxb_2048x64t = jnp.einsum('bsk,bkd->bsd', _ctxb_2048x64c, _ctxb_2048x64P)
        _ctxb_2048x64t = _ctxb_2048x64t * jax.lax.rsqrt(jnp.mean(jnp.square(_ctxb_2048x64t)) + 1e-12) * 0.953939
        ctxb_2048x64 = 0.50053 + 0.288505 * (_ctxb_2048x64t + 0.3 * jax.random.normal(jax.random.fold_in(_rk, 613), (2, 512, 64), jnp.float32))
        _validS = jnp.arange(256)[None, :] < _lenS[:, None]
        _validS2 = jnp.arange(512)[None, :] < _lenS2[:, None]
        _causal = jnp.tril(jnp.ones((256, 256), dtype=bool))
        mask_BxS2_bf1 = jnp.ones((2, 512), dtype=bool)
        return (x, ctx_1024, itok_BxS2_4_31999, ctxb_2048x64, mask_BxS2_bf1)
    x, ctx_1024, itok_BxS2_4_31999, ctxb_2048x64, mask_BxS2_bf1 = _rec_inputs()

    def _L0_xattn_setup():
        import jax, jax.numpy as jnp
        import numpy as np
        B, ST, SM, D, H, F = (2, 256, 256, 128, 16, 512)
        HD = D // H
        EPS = 1e-05

        def _layernorm(x, g, b):
            mu = jnp.mean(x, axis=-1, keepdims=True)
            var = jnp.var(x, axis=-1, keepdims=True)
            return (x - mu) * jax.lax.rsqrt(var + EPS) * g + b

        def _alibi_bias(n_q, n_k, heads, dtype):
            slopes = 2.0 ** (-8.0 * jnp.arange(1, heads + 1, dtype=jnp.float32) / heads)
            dist = jnp.abs(jnp.arange(n_q)[:, None] - jnp.arange(n_k)[None, :]).astype(jnp.float32)
            return (-slopes[:, None, None] * dist).astype(dtype)

        def _sdpa(q, k, v, bias=None):
            scores = jnp.einsum('bhnd,bhmd->bhnm', q, k) / jnp.sqrt(jnp.asarray(HD, q.dtype))
            if bias is not None:
                scores = scores + bias
            attn = jax.nn.softmax(scores, axis=-1)
            return jnp.einsum('bhnm,bhmd->bhnd', attn, v)

        def _split_heads(x):
            b, n, _ = x.shape
            return x.reshape(b, n, H, HD).transpose(0, 2, 1, 3)

        def _merge_heads(x):
            b, h, n, d = x.shape
            return x.transpose(0, 2, 1, 3).reshape(b, n, h * d)
        key = jax.random.key(seed)
        ks = jax.random.split(key, 24)

        def lin_w(k, out_dim, in_dim):
            lim = np.sqrt(6.0 / (in_dim + out_dim))
            return jax.random.uniform(k, (out_dim, in_dim), jnp.float32, -lim, lim)
        return {'tgt': jax.random.normal(ks[0], (B, ST, D), jnp.float32), 'mem': jax.random.normal(ks[1], (B, SM, D), jnp.float32), 'qkv_w': lin_w(ks[2], 3 * D, D), 'qkv_b': jnp.zeros((3 * D,)), 'self_out_w': lin_w(ks[3], D, D), 'self_out_b': jnp.zeros((D,)), 'q_w': lin_w(ks[4], D, D), 'q_b': jnp.zeros((D,)), 'kv_w': lin_w(ks[5], 2 * D, D), 'kv_b': jnp.zeros((2 * D,)), 'cross_out_w': lin_w(ks[6], D, D), 'cross_out_b': jnp.zeros((D,)), 'w12': lin_w(ks[7], 2 * F, D), 'b12': jnp.zeros((2 * F,)), 'w3': lin_w(ks[8], D, F), 'b3': jnp.zeros((D,)), 'ln1_g': jnp.ones((D,)), 'ln1_b': jnp.zeros((D,)), 'ln2_g': jnp.ones((D,)), 'ln2_b': jnp.zeros((D,)), 'ln3_g': jnp.ones((D,)), 'ln3_b': jnp.zeros((D,))}
    _L0_xattn_all = _L0_xattn_setup()
    _L0_xattn_in = {k: v for k, v in _L0_xattn_all.items() if k in ('qkv_w', 'qkv_b', 'self_out_w', 'self_out_b', 'q_w', 'q_b', 'kv_w', 'kv_b', 'cross_out_w', 'cross_out_b', 'w12', 'b12', 'w3', 'b3', 'ln1_g', 'ln1_b', 'ln2_g', 'ln2_b', 'ln3_g', 'ln3_b')}
    del _L0_xattn_all

    def _L1_xattn_setup():
        import jax, jax.numpy as jnp
        import numpy as np
        BATCH, T, H, S, P, NH = (4, 256, 128, 64, 64, 8)
        HD = H // NH

        def _layernorm(x, g, b):
            mu = jnp.mean(x, axis=-1, keepdims=True)
            var = jnp.mean((x - mu) ** 2, axis=-1, keepdims=True)
            return (x - mu) * jax.lax.rsqrt(var + 1e-05) * g + b

        def _mha(q_in, kv_in, W_qkv, b_qkv, W_o, b_o):
            Wq, Wk, Wv = jnp.split(W_qkv, 3, axis=0)
            bq, bk, bv = jnp.split(b_qkv, 3, axis=0)

            def heads(x, W, b):
                y = x @ W.T + b
                return y.reshape(y.shape[0], y.shape[1], NH, HD).transpose(0, 2, 1, 3)
            q, k, v = (heads(q_in, Wq, bq), heads(kv_in, Wk, bk), heads(kv_in, Wv, bv))
            scores = jnp.einsum('bhqd,bhkd->bhqk', q, k) * (1.0 / np.sqrt(HD))
            attn = jax.nn.softmax(scores, axis=-1)
            out = jnp.einsum('bhqk,bhkd->bhqd', attn, v)
            out = out.transpose(0, 2, 1, 3).reshape(q_in.shape)
            return out @ W_o.T + b_o
        key = jax.random.key(seed)
        ks = jax.random.split(key, 16)
        sH = 1.0 / np.sqrt(H)
        d = {}
        d['builder_state'] = jax.random.normal(ks[0], (BATCH, T, H), jnp.float32)
        d['base_state'] = jax.random.normal(ks[1], (BATCH, T, H), jnp.float32)
        d['input_ids'] = jax.random.randint(ks[2], (BATCH, T), 0, 4000)
        d['program_probs'] = jax.random.uniform(ks[3], (BATCH, T, P), jnp.float32)
        d['A'] = jax.random.normal(ks[4], (S, S), jnp.float32) * (0.5 / np.sqrt(S))
        d['Bmat'] = jax.random.normal(ks[5], (H, S), jnp.float32) * sH
        d['Cmat'] = jax.random.normal(ks[6], (S, H), jnp.float32) * (1.0 / np.sqrt(S))
        d['W_in'] = jax.random.normal(ks[7], (H, H), jnp.float32) * sH
        d['b_in'] = jnp.zeros((H,), jnp.float32)
        d['W_qkv'] = jax.random.normal(ks[8], (3 * H, H), jnp.float32) * sH
        d['b_qkv'] = jnp.zeros((3 * H,), jnp.float32)
        d['W_o'] = jax.random.normal(ks[9], (H, H), jnp.float32) * sH
        d['b_o'] = jnp.zeros((H,), jnp.float32)
        d['W_prog'] = jax.random.normal(ks[10], (H, P), jnp.float32) * (1.0 / np.sqrt(P))
        d['b_prog'] = jnp.zeros((H,), jnp.float32)
        d['g1'] = jnp.ones((H,), jnp.float32)
        d['beta1'] = jnp.zeros((H,), jnp.float32)
        d['g2'] = jnp.ones((H,), jnp.float32)
        d['beta2'] = jnp.zeros((H,), jnp.float32)
        return d
    _L1_xattn_all = _L1_xattn_setup()
    _L1_xattn_in = {k: v for k, v in _L1_xattn_all.items() if k in ('A', 'Bmat', 'Cmat', 'W_in', 'b_in', 'W_qkv', 'b_qkv', 'W_o', 'b_o', 'W_prog', 'b_prog', 'g1', 'beta1', 'g2', 'beta2')}
    del _L1_xattn_all

    def _L2_xattn_setup():
        import jax, jax.numpy as jnp
        import numpy as np
        H = 16
        EPS = 1e-05

        def _ln(x, g, b):
            m = x.mean(-1, keepdims=True)
            v = x.var(-1, keepdims=True)
            return (x - m) / jnp.sqrt(v + EPS) * g + b

        def _heads(x):
            b, s, d = x.shape
            return x.reshape(b, s, H, d // H).transpose(0, 2, 1, 3)

        def _merge_buggy(z):
            b, h, s, dh = z.shape
            return z.reshape(b, s, h * dh)

        def _attn(q_in, kv_in, resid, wq, bq, wk, bk, wv, bv, g, be, scale_by_seq, apply_triu):
            q = _heads(q_in @ wq + bq)
            k = _heads(kv_in @ wk + bk)
            v = _heads(kv_in @ wv + bv)
            qk = jnp.einsum('bhqd,bhkd->bhqk', q, k)
            qk = jnp.where(jnp.isnan(qk), -jnp.inf, qk)
            if scale_by_seq:
                qk = qk / jnp.sqrt(jnp.asarray(qk.shape[-1], qk.dtype))
            a = jax.nn.softmax(qk, axis=-1)
            a = jnp.where(jnp.isnan(a), 0.0, a)
            v = jnp.where(jnp.isnan(v), 0.0, v)
            if apply_triu:
                s = a.shape[-1]
                a = a * jnp.triu(jnp.ones((s, s), a.dtype))
            z = jnp.einsum('bhqk,bhkd->bhqd', a, v)
            z = _merge_buggy(z)
            return _ln(resid + z, g, be)
        key = jax.random.key(seed)
        ks = jax.random.split(key, 20)
        B, S, D, F = (2, 256, 128, 128)
        p = lambda k, sh: jax.random.normal(k, sh, jnp.float32) * 0.02
        inp = {'encoded': jax.random.normal(ks[0], (B, S, D), jnp.float32), 'decoded': jax.random.normal(ks[1], (B, S, D), jnp.float32), 'sa_wq': p(ks[2], (D, D)), 'sa_bq': jnp.zeros((D,), jnp.float32), 'sa_wk': p(ks[3], (D, D)), 'sa_bk': jnp.zeros((D,), jnp.float32), 'sa_wv': p(ks[4], (D, D)), 'sa_bv': jnp.zeros((D,), jnp.float32), 'sa_g': jnp.ones((D,), jnp.float32), 'sa_b': jnp.zeros((D,), jnp.float32), 'ca_wq': p(ks[5], (D, D)), 'ca_bq': jnp.zeros((D,), jnp.float32), 'ca_wk': p(ks[6], (D, D)), 'ca_bk': jnp.zeros((D,), jnp.float32), 'ca_wv': p(ks[7], (D, D)), 'ca_bv': jnp.zeros((D,), jnp.float32), 'ca_g': jnp.ones((D,), jnp.float32), 'ca_b': jnp.zeros((D,), jnp.float32), 'ffn_w1': p(ks[8], (D, F)), 'ffn_b1': jnp.zeros((F,), jnp.float32), 'ffn_w2': p(ks[9], (F, D)), 'ffn_b2': jnp.zeros((D,), jnp.float32), 'ffn_g': jnp.ones((D,), jnp.float32), 'ffn_b': jnp.zeros((D,), jnp.float32)}
        return inp
    _L2_xattn_all = _L2_xattn_setup()
    _L2_xattn_in = {k: v for k, v in _L2_xattn_all.items() if k in ('sa_wq', 'sa_bq', 'sa_wk', 'sa_bk', 'sa_wv', 'sa_bv', 'sa_g', 'sa_b', 'ca_wq', 'ca_bq', 'ca_wk', 'ca_bk', 'ca_wv', 'ca_bv', 'ca_g', 'ca_b', 'ffn_w1', 'ffn_b1', 'ffn_w2', 'ffn_b2', 'ffn_g', 'ffn_b')}
    del _L2_xattn_all

    def _L3_xattn_setup():
        import jax, jax.numpy as jnp
        import numpy as np
        EPS = 1e-06
        N_HEADS = 16

        def rmsnorm(x, g):
            return x * jax.lax.rsqrt(jnp.mean(x * x, axis=-1, keepdims=True) + EPS) * g
        key = jax.random.key(seed)
        ks = jax.random.split(key, 8)
        B, Tq, Tc, dq, dc, dm = (2, 256, 256, 128, 128, 128)
        query = jax.random.normal(ks[0], (B, Tq, dq), dtype=jnp.float32)
        context = jax.random.normal(ks[1], (B, Tc, dc), dtype=jnp.float32)
        context_mask = jnp.ones((B, Tc), dtype=bool)
        s = 0.02
        Wq = jax.random.normal(ks[2], (dq, dm), dtype=jnp.float32) * s
        Wk = jax.random.normal(ks[3], (dc, dm), dtype=jnp.float32) * s
        Wv = jax.random.normal(ks[4], (dc, dm), dtype=jnp.float32) * s
        Wo = jax.random.normal(ks[5], (dm, dq), dtype=jnp.float32) * s
        g_q = jnp.ones((dq,), dtype=jnp.float32)
        g_c = jnp.ones((dc,), dtype=jnp.float32)
        g_out = jnp.ones((dq,), dtype=jnp.float32)
        return dict(query=query, context=context, context_mask=context_mask, Wq=Wq, Wk=Wk, Wv=Wv, Wo=Wo, g_q=g_q, g_c=g_c, g_out=g_out)
    _L3_xattn_all = _L3_xattn_setup()
    _L3_xattn_in = {k: v for k, v in _L3_xattn_all.items() if k in ('Wq', 'Wk', 'Wv', 'Wo', 'g_q', 'g_c', 'g_out')}
    del _L3_xattn_all
    return {'x': x, 'ctx_1024': ctx_1024, 'itok_BxS2_4_31999': itok_BxS2_4_31999, 'ctxb_2048x64': ctxb_2048x64, 'mask_BxS2_bf1': mask_BxS2_bf1, 'L0_xattn_qkv_w': _L0_xattn_in['qkv_w'], 'L0_xattn_qkv_b': _L0_xattn_in['qkv_b'], 'L0_xattn_self_out_w': _L0_xattn_in['self_out_w'], 'L0_xattn_self_out_b': _L0_xattn_in['self_out_b'], 'L0_xattn_q_w': _L0_xattn_in['q_w'], 'L0_xattn_q_b': _L0_xattn_in['q_b'], 'L0_xattn_kv_w': _L0_xattn_in['kv_w'], 'L0_xattn_kv_b': _L0_xattn_in['kv_b'], 'L0_xattn_cross_out_w': _L0_xattn_in['cross_out_w'], 'L0_xattn_cross_out_b': _L0_xattn_in['cross_out_b'], 'L0_xattn_w12': _L0_xattn_in['w12'], 'L0_xattn_b12': _L0_xattn_in['b12'], 'L0_xattn_w3': _L0_xattn_in['w3'], 'L0_xattn_b3': _L0_xattn_in['b3'], 'L0_xattn_ln1_g': _L0_xattn_in['ln1_g'], 'L0_xattn_ln1_b': _L0_xattn_in['ln1_b'], 'L0_xattn_ln2_g': _L0_xattn_in['ln2_g'], 'L0_xattn_ln2_b': _L0_xattn_in['ln2_b'], 'L0_xattn_ln3_g': _L0_xattn_in['ln3_g'], 'L0_xattn_ln3_b': _L0_xattn_in['ln3_b'], 'L1_xattn_A': _L1_xattn_in['A'], 'L1_xattn_Bmat': _L1_xattn_in['Bmat'], 'L1_xattn_Cmat': _L1_xattn_in['Cmat'], 'L1_xattn_W_in': _L1_xattn_in['W_in'], 'L1_xattn_b_in': _L1_xattn_in['b_in'], 'L1_xattn_W_qkv': _L1_xattn_in['W_qkv'], 'L1_xattn_b_qkv': _L1_xattn_in['b_qkv'], 'L1_xattn_W_o': _L1_xattn_in['W_o'], 'L1_xattn_b_o': _L1_xattn_in['b_o'], 'L1_xattn_W_prog': _L1_xattn_in['W_prog'], 'L1_xattn_b_prog': _L1_xattn_in['b_prog'], 'L1_xattn_g1': _L1_xattn_in['g1'], 'L1_xattn_beta1': _L1_xattn_in['beta1'], 'L1_xattn_g2': _L1_xattn_in['g2'], 'L1_xattn_beta2': _L1_xattn_in['beta2'], 'L2_xattn_sa_wq': _L2_xattn_in['sa_wq'], 'L2_xattn_sa_bq': _L2_xattn_in['sa_bq'], 'L2_xattn_sa_wk': _L2_xattn_in['sa_wk'], 'L2_xattn_sa_bk': _L2_xattn_in['sa_bk'], 'L2_xattn_sa_wv': _L2_xattn_in['sa_wv'], 'L2_xattn_sa_bv': _L2_xattn_in['sa_bv'], 'L2_xattn_sa_g': _L2_xattn_in['sa_g'], 'L2_xattn_sa_b': _L2_xattn_in['sa_b'], 'L2_xattn_ca_wq': _L2_xattn_in['ca_wq'], 'L2_xattn_ca_bq': _L2_xattn_in['ca_bq'], 'L2_xattn_ca_wk': _L2_xattn_in['ca_wk'], 'L2_xattn_ca_bk': _L2_xattn_in['ca_bk'], 'L2_xattn_ca_wv': _L2_xattn_in['ca_wv'], 'L2_xattn_ca_bv': _L2_xattn_in['ca_bv'], 'L2_xattn_ca_g': _L2_xattn_in['ca_g'], 'L2_xattn_ca_b': _L2_xattn_in['ca_b'], 'L2_xattn_ffn_w1': _L2_xattn_in['ffn_w1'], 'L2_xattn_ffn_b1': _L2_xattn_in['ffn_b1'], 'L2_xattn_ffn_w2': _L2_xattn_in['ffn_w2'], 'L2_xattn_ffn_b2': _L2_xattn_in['ffn_b2'], 'L2_xattn_ffn_g': _L2_xattn_in['ffn_g'], 'L2_xattn_ffn_b': _L2_xattn_in['ffn_b'], 'L3_xattn_Wq': _L3_xattn_in['Wq'], 'L3_xattn_Wk': _L3_xattn_in['Wk'], 'L3_xattn_Wv': _L3_xattn_in['Wv'], 'L3_xattn_Wo': _L3_xattn_in['Wo'], 'L3_xattn_g_q': _L3_xattn_in['g_q'], 'L3_xattn_g_c': _L3_xattn_in['g_c'], 'L3_xattn_g_out': _L3_xattn_in['g_out']}

def reference(x, ctx_1024, itok_BxS2_4_31999, ctxb_2048x64, mask_BxS2_bf1, L0_xattn_qkv_w, L0_xattn_qkv_b, L0_xattn_self_out_w, L0_xattn_self_out_b, L0_xattn_q_w, L0_xattn_q_b, L0_xattn_kv_w, L0_xattn_kv_b, L0_xattn_cross_out_w, L0_xattn_cross_out_b, L0_xattn_w12, L0_xattn_b12, L0_xattn_w3, L0_xattn_b3, L0_xattn_ln1_g, L0_xattn_ln1_b, L0_xattn_ln2_g, L0_xattn_ln2_b, L0_xattn_ln3_g, L0_xattn_ln3_b, L1_xattn_A, L1_xattn_Bmat, L1_xattn_Cmat, L1_xattn_W_in, L1_xattn_b_in, L1_xattn_W_qkv, L1_xattn_b_qkv, L1_xattn_W_o, L1_xattn_b_o, L1_xattn_W_prog, L1_xattn_b_prog, L1_xattn_g1, L1_xattn_beta1, L1_xattn_g2, L1_xattn_beta2, L2_xattn_sa_wq, L2_xattn_sa_bq, L2_xattn_sa_wk, L2_xattn_sa_bk, L2_xattn_sa_wv, L2_xattn_sa_bv, L2_xattn_sa_g, L2_xattn_sa_b, L2_xattn_ca_wq, L2_xattn_ca_bq, L2_xattn_ca_wk, L2_xattn_ca_bk, L2_xattn_ca_wv, L2_xattn_ca_bv, L2_xattn_ca_g, L2_xattn_ca_b, L2_xattn_ffn_w1, L2_xattn_ffn_b1, L2_xattn_ffn_w2, L2_xattn_ffn_b2, L2_xattn_ffn_g, L2_xattn_ffn_b, L3_xattn_Wq, L3_xattn_Wk, L3_xattn_Wv, L3_xattn_Wo, L3_xattn_g_q, L3_xattn_g_c, L3_xattn_g_out):
    import jax
    import jax.numpy as jnp

    def _L0_xattn_ref(tgt, mem, qkv_w, qkv_b, self_out_w, self_out_b, q_w, q_b, kv_w, kv_b, cross_out_w, cross_out_b, w12, b12, w3, b3, ln1_g, ln1_b, ln2_g, ln2_b, ln3_g, ln3_b):
        import jax, jax.numpy as jnp
        import numpy as np
        B, ST, SM, D, H, F = (2, 256, 256, 128, 16, 512)
        HD = D // H
        EPS = 1e-05

        def _layernorm(x, g, b):
            mu = jnp.mean(x, axis=-1, keepdims=True)
            var = jnp.var(x, axis=-1, keepdims=True)
            return (x - mu) * jax.lax.rsqrt(var + EPS) * g + b

        def _alibi_bias(n_q, n_k, heads, dtype):
            slopes = 2.0 ** (-8.0 * jnp.arange(1, heads + 1, dtype=jnp.float32) / heads)
            dist = jnp.abs(jnp.arange(n_q)[:, None] - jnp.arange(n_k)[None, :]).astype(jnp.float32)
            return (-slopes[:, None, None] * dist).astype(dtype)

        def _sdpa(q, k, v, bias=None):
            scores = jnp.einsum('bhnd,bhmd->bhnm', q, k) / jnp.sqrt(jnp.asarray(HD, q.dtype))
            if bias is not None:
                scores = scores + bias
            attn = jax.nn.softmax(scores, axis=-1)
            return jnp.einsum('bhnm,bhmd->bhnd', attn, v)

        def _split_heads(x):
            b, n, _ = x.shape
            return x.reshape(b, n, H, HD).transpose(0, 2, 1, 3)

        def _merge_heads(x):
            b, h, n, d = x.shape
            return x.transpose(0, 2, 1, 3).reshape(b, n, h * d)
        x = tgt
        qkv = x @ qkv_w.T + qkv_b
        q, k, v = jnp.split(qkv, 3, axis=-1)
        q, k, v = (_split_heads(q), _split_heads(k), _split_heads(v))
        bias = _alibi_bias(ST, ST, H, x.dtype)
        sa = _merge_heads(_sdpa(q, k, v, bias)) @ self_out_w.T + self_out_b
        x = _layernorm(x + sa, ln1_g, ln1_b)
        q = _split_heads(x @ q_w.T + q_b)
        kv = mem @ kv_w.T + kv_b
        kx, vx = jnp.split(kv, 2, axis=-1)
        kx, vx = (_split_heads(kx), _split_heads(vx))
        ca = _merge_heads(_sdpa(q, kx, vx)) @ cross_out_w.T + cross_out_b
        x = _layernorm(x + ca, ln2_g, ln2_b)
        h = x @ w12.T + b12
        a, b_ = jnp.split(h, 2, axis=-1)
        ff = jax.nn.silu(a) * b_ @ w3.T + b3
        x = _layernorm(x + ff, ln3_g, ln3_b)
        return x

    def _L1_xattn_ref(builder_state, base_state, input_ids, program_probs, A, Bmat, Cmat, W_in, b_in, W_qkv, b_qkv, W_o, b_o, W_prog, b_prog, g1, beta1, g2, beta2):
        import jax, jax.numpy as jnp
        import numpy as np
        BATCH, T, H, S, P, NH = (4, 256, 128, 64, 64, 8)
        HD = H // NH

        def _layernorm(x, g, b):
            mu = jnp.mean(x, axis=-1, keepdims=True)
            var = jnp.mean((x - mu) ** 2, axis=-1, keepdims=True)
            return (x - mu) * jax.lax.rsqrt(var + 1e-05) * g + b

        def _mha(q_in, kv_in, W_qkv, b_qkv, W_o, b_o):
            Wq, Wk, Wv = jnp.split(W_qkv, 3, axis=0)
            bq, bk, bv = jnp.split(b_qkv, 3, axis=0)

            def heads(x, W, b):
                y = x @ W.T + b
                return y.reshape(y.shape[0], y.shape[1], NH, HD).transpose(0, 2, 1, 3)
            q, k, v = (heads(q_in, Wq, bq), heads(kv_in, Wk, bk), heads(kv_in, Wv, bv))
            scores = jnp.einsum('bhqd,bhkd->bhqk', q, k) * (1.0 / np.sqrt(HD))
            attn = jax.nn.softmax(scores, axis=-1)
            out = jnp.einsum('bhqk,bhkd->bhqd', attn, v)
            out = out.transpose(0, 2, 1, 3).reshape(q_in.shape)
            return out @ W_o.T + b_o
        residual = builder_state
        x = _layernorm(builder_state, g1, beta1)
        base_n = _layernorm(base_state, g1, beta1)
        x = residual + _mha(x, base_n, W_qkv, b_qkv, W_o, b_o)
        residual = x
        xn = _layernorm(x, g2, beta2)
        U = (xn @ W_in.T + b_in) @ Bmat

        def step(s, u_t):
            s = jax.nn.silu(s @ A.T) + u_t
            return (s, s)
        _, states = jax.lax.scan(step, jnp.zeros((builder_state.shape[0], S), U.dtype), U.transpose(1, 0, 2))
        ssm_out = jnp.einsum('tbs,sh->bth', states, Cmat)
        x = residual + ssm_out
        mod = program_probs.mean(axis=1) @ W_prog.T + b_prog
        return x + mod[:, None, :]

    def _L2_xattn_ref(encoded, decoded, sa_wq, sa_bq, sa_wk, sa_bk, sa_wv, sa_bv, sa_g, sa_b, ca_wq, ca_bq, ca_wk, ca_bk, ca_wv, ca_bv, ca_g, ca_b, ffn_w1, ffn_b1, ffn_w2, ffn_b2, ffn_g, ffn_b):
        import jax, jax.numpy as jnp
        import numpy as np
        H = 16
        EPS = 1e-05

        def _ln(x, g, b):
            m = x.mean(-1, keepdims=True)
            v = x.var(-1, keepdims=True)
            return (x - m) / jnp.sqrt(v + EPS) * g + b

        def _heads(x):
            b, s, d = x.shape
            return x.reshape(b, s, H, d // H).transpose(0, 2, 1, 3)

        def _merge_buggy(z):
            b, h, s, dh = z.shape
            return z.reshape(b, s, h * dh)

        def _attn(q_in, kv_in, resid, wq, bq, wk, bk, wv, bv, g, be, scale_by_seq, apply_triu):
            q = _heads(q_in @ wq + bq)
            k = _heads(kv_in @ wk + bk)
            v = _heads(kv_in @ wv + bv)
            qk = jnp.einsum('bhqd,bhkd->bhqk', q, k)
            qk = jnp.where(jnp.isnan(qk), -jnp.inf, qk)
            if scale_by_seq:
                qk = qk / jnp.sqrt(jnp.asarray(qk.shape[-1], qk.dtype))
            a = jax.nn.softmax(qk, axis=-1)
            a = jnp.where(jnp.isnan(a), 0.0, a)
            v = jnp.where(jnp.isnan(v), 0.0, v)
            if apply_triu:
                s = a.shape[-1]
                a = a * jnp.triu(jnp.ones((s, s), a.dtype))
            z = jnp.einsum('bhqk,bhkd->bhqd', a, v)
            z = _merge_buggy(z)
            return _ln(resid + z, g, be)
        x = _attn(decoded, decoded, decoded, sa_wq, sa_bq, sa_wk, sa_bk, sa_wv, sa_bv, sa_g, sa_b, scale_by_seq=True, apply_triu=True)
        x = _attn(x, encoded, x, ca_wq, ca_bq, ca_wk, ca_bk, ca_wv, ca_bv, ca_g, ca_b, scale_by_seq=False, apply_triu=False)
        y = jax.nn.relu(x @ ffn_w1 + ffn_b1) @ ffn_w2 + ffn_b2
        return _ln(y + x, ffn_g, ffn_b)

    def _L3_xattn_ref(query, context, context_mask, Wq, Wk, Wv, Wo, g_q, g_c, g_out):
        import jax, jax.numpy as jnp
        import numpy as np
        EPS = 1e-06
        N_HEADS = 16

        def rmsnorm(x, g):
            return x * jax.lax.rsqrt(jnp.mean(x * x, axis=-1, keepdims=True) + EPS) * g
        B, Tq, _ = query.shape
        Tc = context.shape[1]
        H = N_HEADS
        dm = Wq.shape[1]
        hd = dm // H
        scale = hd ** (-0.5)
        q_norm = rmsnorm(query, g_q)
        c_norm = rmsnorm(context, g_c)
        Q = (q_norm @ Wq).reshape(B, Tq, H, hd).transpose(0, 2, 1, 3)
        K = (c_norm @ Wk).reshape(B, Tc, H, hd).transpose(0, 2, 1, 3)
        V = (c_norm @ Wv).reshape(B, Tc, H, hd).transpose(0, 2, 1, 3)
        scores = jnp.einsum('bhqd,bhkd->bhqk', Q, K) * scale
        scores = jnp.where(context_mask[:, None, None, :], scores, -jnp.inf)
        attn = jax.nn.softmax(scores, axis=-1)
        attn = jnp.nan_to_num(attn, nan=0.0)
        out = jnp.einsum('bhqk,bhkd->bhqd', attn, V)
        out = out.transpose(0, 2, 1, 3).reshape(B, Tq, dm)
        out = out @ Wo
        return rmsnorm(query + out, g_out)
    x = _L0_xattn_ref(x, ctx_1024, L0_xattn_qkv_w, L0_xattn_qkv_b, L0_xattn_self_out_w, L0_xattn_self_out_b, L0_xattn_q_w, L0_xattn_q_b, L0_xattn_kv_w, L0_xattn_kv_b, L0_xattn_cross_out_w, L0_xattn_cross_out_b, L0_xattn_w12, L0_xattn_b12, L0_xattn_w3, L0_xattn_b3, L0_xattn_ln1_g, L0_xattn_ln1_b, L0_xattn_ln2_g, L0_xattn_ln2_b, L0_xattn_ln3_g, L0_xattn_ln3_b)
    x = _L1_xattn_ref(x, ctx_1024, itok_BxS2_4_31999, ctxb_2048x64, L1_xattn_A, L1_xattn_Bmat, L1_xattn_Cmat, L1_xattn_W_in, L1_xattn_b_in, L1_xattn_W_qkv, L1_xattn_b_qkv, L1_xattn_W_o, L1_xattn_b_o, L1_xattn_W_prog, L1_xattn_b_prog, L1_xattn_g1, L1_xattn_beta1, L1_xattn_g2, L1_xattn_beta2)
    x = _L2_xattn_ref(ctx_1024, x, L2_xattn_sa_wq, L2_xattn_sa_bq, L2_xattn_sa_wk, L2_xattn_sa_bk, L2_xattn_sa_wv, L2_xattn_sa_bv, L2_xattn_sa_g, L2_xattn_sa_b, L2_xattn_ca_wq, L2_xattn_ca_bq, L2_xattn_ca_wk, L2_xattn_ca_bk, L2_xattn_ca_wv, L2_xattn_ca_bv, L2_xattn_ca_g, L2_xattn_ca_b, L2_xattn_ffn_w1, L2_xattn_ffn_b1, L2_xattn_ffn_w2, L2_xattn_ffn_b2, L2_xattn_ffn_g, L2_xattn_ffn_b)
    x = _L3_xattn_ref(x, ctx_1024, mask_BxS2_bf1, L3_xattn_Wq, L3_xattn_Wk, L3_xattn_Wv, L3_xattn_Wo, L3_xattn_g_q, L3_xattn_g_c, L3_xattn_g_out)
    return x

_drawn_inputs = setup_inputs


def setup_inputs(seed=0):
    import zlib

    import numpy as np

    out = dict(_drawn_inputs(seed))
    spreads = {'L0_xattn_qkv_b': (0.0, 0.1),
     'L0_xattn_self_out_b': (0.0, 0.1),
     'L0_xattn_q_b': (0.0, 0.654),
     'L0_xattn_kv_b': (0.0, 0.1),
     'L0_xattn_cross_out_b': (0.0, 0.1),
     'L0_xattn_b12': (0.0, 0.1),
     'L0_xattn_b3': (0.0, 0.1),
     'L0_xattn_ln1_g': (1.0, 0.2),
     'L0_xattn_ln1_b': (0.0, 0.1),
     'L0_xattn_ln2_g': (1.0, 0.2),
     'L0_xattn_ln2_b': (0.0, 0.1),
     'L0_xattn_ln3_g': (1.0, 0.2),
     'L0_xattn_ln3_b': (0.0, 0.1),
     'L1_xattn_b_in': (0.0, 0.1),
     'L1_xattn_b_qkv': (0.0, 0.1),
     'L1_xattn_b_o': (0.0, 0.1),
     'L1_xattn_b_prog': (0.0, 0.1),
     'L1_xattn_g1': (1.0, 0.2),
     'L1_xattn_beta1': (0.0, 0.1),
     'L1_xattn_g2': (1.0, 0.2),
     'L1_xattn_beta2': (0.0, 0.1),
     'L2_xattn_sa_bq': (0.0, 0.8),
     'L2_xattn_sa_bk': (0.0, 0.8),
     'L2_xattn_sa_bv': (0.0, 0.1),
     'L2_xattn_sa_g': (1.0, 0.2),
     'L2_xattn_sa_b': (0.0, 0.1),
     'L2_xattn_ca_bq': (0.0, 0.8),
     'L2_xattn_ca_bk': (0.0, 0.8),
     'L2_xattn_ca_bv': (0.0, 0.1),
     'L2_xattn_ca_g': (1.0, 0.2),
     'L2_xattn_ca_b': (0.0, 0.1),
     'L2_xattn_ffn_b1': (0.0, 0.603),
     'L2_xattn_ffn_b2': (0.0, 0.1),
     'L2_xattn_ffn_g': (1.0, 0.2),
     'L2_xattn_ffn_b': (0.0, 0.1),
     'L3_xattn_g_q': (1.0, 0.6),
     'L3_xattn_g_c': (1.0, 0.6),
     'L3_xattn_g_out': (1.0, 0.2)}
    factors = {'L2_xattn_sa_wq': 8.0,
     'L2_xattn_sa_wk': 8.0,
     'L2_xattn_ca_wq': 8.0,
     'L2_xattn_ca_wk': 8.0,
     'L3_xattn_Wq': 8.0,
     'L3_xattn_Wk': 8.0}
    for name, (base, spread) in spreads.items():
        noise = np.random.default_rng([zlib.crc32(name.encode()), seed]).standard_normal(out[name].shape)
        drawn = base * np.exp(spread * noise) if base else spread * noise
        out[name] = jnp.asarray(drawn.astype(out[name].dtype))
    for name, factor in factors.items():
        out[name] = (out[name] * factor).astype(out[name].dtype)
    return out
```

```python
from contextlib import ExitStack

import numpy as np

import concourse.bass as bass
from concourse import mybir

ALU = mybir.AluOpType
ACT = mybir.ActivationFunctionType
AX_X = mybir.AxisListType.X
F32 = mybir.dt.float32
BF16 = mybir.dt.bfloat16
U8 = mybir.dt.uint8

B, T, D = 2, 256, 128
S2 = 512
QT = T // 128
S_STATE, P_PROG, F_FF = 64, 64, 512
BIG = 1e30
PARTS = 3
TERM_ROWS = 96
MASK_ROW = 48
TERMS = 6
Q_TERM = [0, 0, 0, 1, 1, 2]
K_TERM = [0, 1, 2, 0, 1, 0]

HEADS = [16, 16, 8, 16, 16, 16]
KEYS = [T, S2, S2, T, S2, S2]
SA0, CA0, CA1, SA2, CA2, CA3 = range(6)
SCALE = [8 ** -0.5, 8 ** -0.5, 0.25, 1.0 / 16.0, 1.0, 8 ** -0.5]
UNITS = [(layer, b) for layer in range(6) for b in range(B)]

W_COLS = {}
_at = 0
for _n, _w in [("q0", 128), ("k0", 128), ("v0", 128), ("o0", 128), ("q1", 128), ("k1", 128), ("v1", 128), ("o1", 128),
               ("w12", 1024), ("w3", 512), ("q2", 128), ("k2", 128), ("v2", 128), ("o2", 128), ("win", 128),
               ("bmat", 64), ("at", 64), ("cmat", 128), ("prog", 128), ("q3", 128), ("k3", 128), ("v3", 128),
               ("q4", 128), ("k4", 128), ("v4", 128), ("f1", 128), ("f2", 128), ("q5", 128), ("k5", 128),
               ("v5", 128), ("o5", 128)]:
    W_COLS[_n] = (_at, _w)
    _at += _w
W_TOTAL = _at
W_FIRST = 384
COLS = ["bq0", "bk0", "bq1", "bk1", "bq2", "bk2", "bq3", "bk3", "bq4", "bk4", "g_ln1", "b_ln1", "g_ln2", "b_ln2",
        "g_x1", "b_x1", "g_x2", "b_x2", "b_in", "g_sa", "b_sa", "g_ca", "b_ca", "b_f1", "g_q", "g_c"] + \
       [f"b12_{i}" for i in range(8)]
COL = {n: i for i, n in enumerate(COLS)}
ROWS = ["bv0", "bo0", "bv1", "bo1", "b3", "bv2", "bo2", "bprog", "bv3", "bv4", "bf2"]
ROW = {n: i for i, n in enumerate(ROWS)}
TOKS = ["g_ln1", "b_ln1", "g_ln2", "b_ln2", "g_ln3", "b_ln3", "g_sa", "b_sa", "g_ca", "b_ca", "g_ffn", "b_ffn", "g_out"]
TOK = {n: i for i, n in enumerate(TOKS)}


def bf16_parts(x):
    parts = []
    x = np.float32(x)
    for _ in range(PARTS):
        p = np.float32((np.array(x, np.float32).view(np.uint32) & np.uint32(0xFFFF0000)).view(np.float32))
        if p != 0:
            parts.append(float(p))
        x = np.float32(x - p)
    return parts


SLOPES = (2.0 ** (-8.0 * np.arange(1, 17, dtype=np.float32) / 16)).astype(np.float32)
SLOPE_PARTS = [(h, p) for h in range(16) for p in bf16_parts(SLOPES[h])]
SLOPE_OF = [[n for n, (hh, _) in enumerate(SLOPE_PARTS) if hh == h] for h in range(16)]

GROUPS = [(u, g) for u, (layer, _) in enumerate(UNITS) for g in range(HEADS[layer] // 4)]
GROUP_AT = {ug: gi for gi, ug in enumerate(GROUPS)}
STEPS = [(gi, kt) for gi, (u, _) in enumerate(GROUPS) for kt in range(KEYS[UNITS[u][0]] // 128)]
STEP_AT = {s: n for n, s in enumerate(STEPS)}
LAG = 2
RING = 3


def last_step(u):
    return max(n for n, (gi, _) in enumerate(STEPS) if GROUPS[gi][0] == u) + 1


def tiles(gi):
    n = S2 // KEYS[UNITS[GROUPS[gi][0]][0]]
    return [(qt, j, n) for qt in range(QT) for j in range(0, 4, n)]


def chain(u):
    layer = UNITS[u][0]
    norm = lambda tag: [("stats", u, tag), ("pow", u, tag), ("norm", u, tag)]
    nxt = u + 2
    query = [("qproj", nxt), ("qsplit", nxt), ("qstore", nxt), ("qload", nxt)]
    if layer == SA0:
        return [("attnT", u), ("oproj", u)] + norm("a") + [("nT", u, "a"), ("tok", u, "a")] + query
    if layer == CA0:
        return ([("attnT", u), ("oproj", u)] + norm("a") + [("nT", u, "a"), ("tok", u, "a")]
                + [("glu", u, f) for f in range(4)] + [("ffout", u)] + norm("b") + [("tokd", u, "b")]
                + norm("c") + [("nT", u, "c")] + query)
    if layer == CA1:
        return [("attnT", u), ("oproj", u)] + norm("a") + [("nT", u, "a"), ("win", u), ("uproj", u)]
    if layer == SA2:
        return [("zstore", u), ("zload", u), ("zadd", u)] + norm("a") + [("nT", u, "a"), ("tok", u, "a")] + query
    if layer == CA2:
        return ([("zstore", u), ("zload", u), ("zadd", u)] + norm("a") + [("nT", u, "a"), ("tok", u, "a"), ("relu", u), ("ffout", u)]
                + norm("b") + [("tokd", u, "b")] + norm("c") + [("nT", u, "c")] + query)
    return [("attnT", u), ("oproj", u)] + norm("a") + [("outmul", u), ("outstore", u)]


def keys_values(u):
    return [("kproj", u), ("ksplit", u), ("kstore", u), ("kload", u), ("vproj", u)]


def context(u):
    return [("cnorm", u), ("cT", u)] + keys_values(u)


def interleave(*lists):
    placed = [((i + 0.5) / len(x), n, i, item) for n, x in enumerate(lists) for i, item in enumerate(x)]
    return [p[3] for p in sorted(placed, key=lambda p: p[:3])]


def schedule():
    out = []
    for u in (0, 1):
        out += [("qproj", u), ("qsplit", u), ("kproj", u), ("ksplit", u), ("qstore", u), ("kstore", u), ("vproj", u), ("qload", u), ("kload", u)]
    waiting = {}
    ends = {u: GROUP_AT[(u, HEADS[UNITS[u][0]] // 4 - 1)] for u in range(len(UNITS))}
    starts = {u: GROUP_AT[(u, 0)] for u in range(len(UNITS))}
    scan_at = starts[2 * SA2]
    extra = {starts[0]: keys_values(2), starts[1]: [("ctxstats",)] + keys_values(3),
             starts[2]: context(4) + [("mod1",), ("mod2",)], starts[3]: context(5),
             starts[4] + 1: keys_values(8), starts[5] + 1: keys_values(9),
             starts[7]: [("maskprep",), ("flag",)], starts[7] + 1: context(10), starts[8]: context(11)}
    n_slots = len(GROUPS)
    for slot in range(n_slots + LAG):
        if slot == scan_at:
            rest = [x for gi in range(slot - LAG, slot) for x in steps_of(gi) + [("finish", gi)]]
            out += interleave(rest, waiting.pop(2 * CA1)) + chain(2 * CA1 + 1)
            out += [("scan",)]
            for b in range(B):
                u = 2 * SA2 + b
                out += [("ssm", b), ("xT", b), ("qproj", u), ("qsplit", u), ("kproj", u), ("ksplit", u), ("qstore", u), ("kstore", u),
                        ("vproj", u), ("qload", u), ("kload", u)]
        a = [("scores", slot, i) for i in range(len(tiles(slot)))] if slot < n_slots else []
        m = [("shift", slot - 1)] if 0 < slot <= n_slots and slot != scan_at else []
        gb = slot - LAG
        bs = steps_of(gb) if gb >= 0 and not (scan_at - LAG <= gb < scan_at) else []
        if bs:
            bs = bs + [("finish", gb)]
        if slot == scan_at:
            bs = []
        if slot < n_slots:
            u = GROUPS[slot][0]
            if slot == starts[u]:
                for key in [k for k in waiting if k == u - 2]:
                    out += waiting.pop(key)
        ch = []
        for key in sorted(waiting):
            items = waiting[key]
            left = (starts[key + 2] - slot) if key + 2 < len(UNITS) else 1
            take = len(items) if left <= 1 else -(-len(items) // left)
            ch.append(items[:take])
            waiting[key] = items[take:]
        waiting = {k: v for k, v in waiting.items() if v}
        ex = extra.get(slot, [])
        out += m[:0] + interleave(*[x for x in [a, bs, *ch, ex, m] if x])
        if slot + 1 == scan_at:
            out += [("shift", slot)]
        if gb >= 0 and bs:
            u = GROUPS[gb][0]
            if gb == ends[u]:
                waiting[u] = chain(u)
    for key in sorted(waiting):
        out += waiting[key]
    return out


def steps_of(gi):
    n_kt = KEYS[UNITS[GROUPS[gi][0]][0]] // 128
    out = []
    for kt in range(n_kt):
        out.append(("step", STEP_AT[(gi, kt)]))
        if kt:
            out.append(("values", STEP_AT[(gi, kt - 1)]))
    return out + [("values", STEP_AT[(gi, n_kt - 1)])]


SCHED = schedule()
IN_RING = {"scores", "shift", "finish", "attnT", "oproj", "nT", "qproj", "kproj", "vproj", "glu", "ffout", "relu",
           "win", "uproj", "ssm", "xT", "cT", "mod1", "mod2", "flag"}
BANK = {}
_uses = [0] * RING
for _i in SCHED:
    if _i[0] in IN_RING:
        assert _i not in BANK, _i
        _k = len(BANK) % RING
        BANK[_i] = (_k, _uses[_k])
        _uses[_k] += 1
IN_CHAIN = {"stats", "pow", "norm", "tokd", "qsplit", "zadd", "outmul"}
CHAIN = {}
_n = [0] * B
for _i in SCHED:
    if _i[0] in IN_CHAIN:
        _b = UNITS[_i[1]][1]
        _n[_b] += 1
        CHAIN[_i] = _n[_b]
SIDE = {}
_n = [0] * B
for _i in SCHED:
    if _i[0] == "tok":
        _b = UNITS[_i[1]][1]
        _n[_b] += 1
        SIDE[_i] = _n[_b]
KSPLITS = [i[1] for i in SCHED if i[0] == "ksplit"]
CNORMS = [i[1] for i in SCHED if i[0] == "cnorm"]

NORM_COLS = {(SA0, "a"): ("g_ln1", "b_ln1"), (CA0, "a"): ("g_ln2", "b_ln2"), (CA0, "c"): ("g_x1", "b_x1"),
             (CA1, "a"): ("g_x2", "b_x2"), (SA2, "a"): ("g_sa", "b_sa"), (CA2, "a"): ("g_ca", "b_ca"),
             (CA2, "c"): ("g_q", None)}
NORM_TOKS = {(SA0, "a"): ("g_ln1", "b_ln1"), (CA0, "a"): ("g_ln2", "b_ln2"), (CA0, "b"): ("g_ln3", "b_ln3"),
             (SA2, "a"): ("g_sa", "b_sa"), (CA2, "a"): ("g_ca", "b_ca"), (CA2, "b"): ("g_ffn", "b_ffn")}
RMS = {(CA2, "c"), (CA3, "a")}
FROM_X = {(CA0, "c"), (CA1, "a"), (CA2, "c")}
EPS = {True: 1e-6, False: 1e-5}


def build_program(nc, x_tok, x_t, ctx_tok, ctx_t, probs, mask, w, cols, rows, toks, ident, dist, slopes, tri, qones, out):
    with ExitStack() as stack:
        def sb(name, shape, dt=F32):
            return stack.enter_context(nc.sbuf_tensor(name, shape, dt))

        def sem(name):
            return stack.enter_context(nc.semaphore(name))

        w_sb = sb("w_sb", [128, W_TOTAL])
        col_sb = sb("col_sb", [128, len(COLS)])
        row_sb = sb("row_sb", [1, len(ROWS), 128])
        tok_sb = sb("tok_sb", [128, len(TOKS), 128])
        id_sb = sb("id_sb", [128, 128])
        idb_sb = sb("idb_sb", [128, 128], BF16)
        dist_sb = sb("dist_sb", [128, 2, T], BF16)
        tri_sb = sb("tri_sb", [128, 128])
        ones_row = sb("ones_row", [1, 128])
        inv_col = sb("inv_col", [128, 1])
        xT_in = sb("xT_in", [128, B, T])
        ctxT_sb = sb("ctxT_sb", [128, B, S2])
        ctx_sb = sb("ctx_sb", [128, B, 4, 128])
        probs_sb = sb("probs_sb", [128, B, 4, P_PROG])
        mask_sb = sb("mask_sb", [1, B, S2], U8)
        flag_row = sb("flag_row", [1, B])
        flag = sb("flag", [128, B])
        pmean = sb("pmean", [P_PROG, B])
        modrow = sb("modrow", [1, B, 128])
        q_pack = [sb(f"q_pack{b}", [128, 16 * T], BF16) for b in range(B)]
        k_even = [sb(f"k_even{b}", [128, 16 * S2], BF16) for b in range(B)]
        k_odd = [sb(f"k_odd{b}", [128, 16 * S2], BF16) for b in range(B)]
        slope_sb = k_odd[0][:, 8 * S2:8 * S2 + len(SLOPE_PARTS) * 128].rearrange("p (n c) -> p n c", c=128)
        v_self = [sb(f"v_self{b}", [128, 2 * 16 * 16]) for b in range(B)]
        v_even = [sb(f"v_even{b}", [128, 4 * 16 * 16]) for b in range(B)]
        v_odd = [sb(f"v_odd{b}", [128, 4 * 16 * 16]) for b in range(B)]
        den_sb = sb("den_sb", [128, 16])
        probs_e = [sb(f"probs_e{i}", [128, 4 * T]) for i in range(3)]
        probs_m = [sb(f"probs_m{i}", [128, 4, 128]) for i in range(2)]
        rowmax = [sb(f"rowmax{i}", [128, QT, 4]) for i in range(2)]
        shift_p = [sb(f"shift_p{i}", [128, QT, 2, 4], BF16) for i in range(2)]
        shift_t = [sb(f"shift_t{i}", [8, T], BF16) for i in range(4)]
        o_sb = [sb(f"o_sb{i}", [128, T]) for i in range(2)]
        rden = sb("rden", [128, QT, 4, 1])
        X = [sb(f"X{b}", [128, QT, D]) for b in range(B)]
        r = [sb(f"r{b}", [128, QT, D]) for b in range(B)]
        nrm = [sb(f"nrm{b}", [128, QT, D]) for b in range(B)]
        attn = [sb(f"attn{b}", [128, QT, D]) for b in range(B)]
        XT = [sb(f"XT{b}", [128, T]) for b in range(B)]
        z = [sb(f"z{b}", [128, QT, D]) for b in range(B)]
        attnT = [z[b][:, :, :].rearrange("p t d -> p (t d)") for b in range(B)]
        qf = [sb(f"qf{b}", [128, T]) for b in range(B)]
        qr = [sb(f"qr{b}", [128, T]) for b in range(B)]
        glu_t, glu_a, glu_w = attnT, qf, qr
        qp = [sb(f"qp{b}", [128, PARTS, T], BF16) for b in range(B)]
        kf = sb("kf", [128, S2])
        kp = [sb(f"kp{i}", [128, PARTS, S2], BF16) for i in range(2)]
        stats = [sb(f"stats{b}", [128, QT, 6]) for b in range(B)]
        mv = [sb(f"mv{b}", [128, QT, 2]) for b in range(B)]
        ve = [sb(f"ve{b}", [128, QT]) for b in range(B)]
        rs = [sb(f"rs{b}", [128, QT]) for b in range(B)]
        half = sb("half", [128, 8])
        half_b = sb("half_b", [128, 4])
        cstats = sb("cstats", [128, 8, 6])
        cmv = sb("cmv", [128, 8, 2])
        cve = sb("cve", [128, 2, 8])
        crs = sb("crs", [128, 2, 8])
        cn = sb("cn", [128, 4, 128])
        cT = sb("cT", [128, S2])
        hT = sb("hT", [128, 4, T])
        mrow = w_sb[0:1, 0:B * S2 // 2].bitcast(BF16).rearrange("p (b t) -> p b t", b=B)
        UT = w_sb[0:S_STATE, 1024:1024 + T * B].rearrange("p (t b) -> p t b", b=B)
        G = w_sb[0:S_STATE, 1536:1536 + T * B].rearrange("p (t b) -> p t b", b=B)

        ring = [stack.enter_context(nc.psum_tensor(f"ring{k}", [128, 512], F32)) for k in range(RING)]
        st_ps = [stack.enter_context(nc.psum_tensor(f"st_ps{i}", [128, 1024], F32)) for i in range(2)]
        o_ps = stack.enter_context(nc.psum_tensor("o_ps", [128, 512], F32))
        scan_ps = st_ps[0][0:S_STATE, 0:512]

        q_dram = [nc.dram_tensor(f"q_scratch{u}", (128, PARTS, T), BF16).ap() for u in range(12)]
        k_dram = [nc.dram_tensor(f"k_scratch{u}", (128, PARTS, KEYS[UNITS[u][0]]), BF16).ap() for u in range(12)]
        z_dram = {u: nc.dram_tensor(f"z_scratch{u}", (16, T, 8), F32).ap() for u in range(12) if UNITS[u][0] in (SA2, CA2)}

        in_first = sem("in_first")
        in_const = sem("in_const")
        in_ctx = sem("in_ctx")
        in_rest = sem("in_rest")
        consts_set = sem("consts_set")
        idb_done = sem("idb_done")
        packs_set = sem("packs_set")
        kones_set = sem("kones_set")
        ones_cleared = sem("ones_cleared")
        bank_full = [sem(f"bank_full{k}") for k in range(RING)]
        bank_free = [sem(f"bank_free{k}") for k in range(RING)]
        chain_s = [sem(f"chain{b}") for b in range(B)]
        side_s = [sem(f"side{b}") for b in range(B)]
        dve_step = sem("dve_step")
        pool_step = sem("pool_step")
        q_stored = [sem(f"q_stored{u}") for u in range(12)]
        q_landed = [sem(f"q_landed{u}") for u in range(12)]
        k_stored = [sem(f"k_stored{u}") for u in range(12)]
        k_landed = [sem(f"k_landed{u}") for u in range(12)]
        z_stored = {u: sem(f"z_stored{u}") for u in z_dram}
        z_landed = {u: sem(f"z_landed{u}") for u in z_dram}
        keys_split = sem("keys_split")
        shift_ready = sem("shift_ready")
        shift_landed = [sem(f"shift_landed{i}") for i in range(4)]
        st_full = sem("st_full")
        exp_done = sem("exp_done")
        masked = sem("masked")
        values_done = sem("values_done")
        o_taken = sem("o_taken")
        gate_done = sem("gate_done")
        cstats_done = sem("cstats_done")
        crs_done = sem("crs_done")
        cn_done = sem("cn_done")
        mask_done = sem("mask_done")
        scan_pre = sem("scan_pre")
        scan_h = sem("scan_h")
        scan_g = sem("scan_g")
        states_done = sem("states_done")
        out_landed = sem("out_landed")

        def W(name, k=128):
            at, n = W_COLS[name]
            return w_sb[0:k, at:at + n]

        def C(name):
            return col_sb[:, COL[name]:COL[name] + 1]

        def v_pack(u):
            layer, b = UNITS[u]
            t = (v_self if layer in (SA0, SA2) else v_even if layer in (CA0, CA2) else v_odd)[b]
            return t[:, :].rearrange("p (t h c) -> p t h c", h=HEADS[layer], c=16 if HEADS[layer] == 16 else 32)

        def k_rows(u, first, end):
            layer, b = UNITS[u]
            if layer in (SA0, SA2):
                return k_odd[1][first:end, b * 16 * T:(b + 1) * 16 * T]
            return (k_odd if layer in (CA1, CA3) else k_even)[b][first:end, :]

        def q_rows(u, first, end):
            return q_pack[UNITS[u][1]][first:end, :]

        def head_dim(u):
            return D // HEADS[UNITS[u][0]]

        def claim(e, key):
            k, n = BANK[key]
            if n:
                e.wait_ge(bank_free[k], n)
            return ring[k]

        def filled(e, key):
            k, n = BANK[key]
            e.wait_ge(bank_full[k], n + 1)
            return ring[k]

        def taken(e, key):
            k, n = BANK[key]
            e.wait_ge(bank_free[k], n + 1)

        def full(key):
            return bank_full[BANK[key][0]]

        def free(key):
            return bank_free[BANK[key][0]]

        def chained(e, key):
            e.wait_ge(chain_s[UNITS[key[1]][1]], CHAIN[key])

        def source_ready(e, u):
            layer, b = UNITS[u]
            if layer == SA0:
                e.wait_ge(in_first, 64)
            elif layer == SA2:
                taken(e, ("xT", b))
            else:
                taken(e, ("nT", u - 2, {CA0: "a", CA1: "c", CA2: "a", CA3: "c"}[layer]))

        def query_source(u):
            layer, b = UNITS[u]
            return xT_in[:, b, :] if layer == SA0 else XT[b][:, :]

        def key_source(e, u):
            layer, b = UNITS[u]
            if layer in (SA0, SA2):
                source_ready(e, u)
                return query_source(u)
            if layer in (CA0, CA2):
                e.wait_ge(in_ctx, 16)
                return ctxT_sb[:, b, :]
            taken(e, ("cT", u))
            return cT[:, :]

        block = stack.enter_context(nc.Block())

        @block.sync
        def _(sp):
            sp.dma_start(w_sb[:, 0:W_FIRST], w[:, 0:W_FIRST]).then_inc(in_first, 16)
            sp.dma_start(xT_in[:, :, :], x_t).then_inc(in_first, 16)
            sp.dma_start(col_sb[:, :], cols).then_inc(in_first, 16)
            sp.dma_start(row_sb[:, :, :], rows).then_inc(in_first, 16)
            sp.dma_start(dist_sb[:, :, :], dist).then_inc(in_const, 16)
            sp.dma_start(slope_sb, slopes).then_inc(in_const, 16)
            sp.dma_start(id_sb[:, :], ident).then_inc(in_const, 16)
            sp.dma_start(ctxT_sb[:, :, :], ctx_t).then_inc(in_ctx, 16)
            sp.dma_start(w_sb[:, W_FIRST:W_TOTAL], w[:, W_FIRST:W_TOTAL]).then_inc(in_rest, 16)
            for b in range(B):
                sp.dma_start(X[b][:, :, :], x_tok[b]).then_inc(in_rest, 16)
            sp.dma_start(tok_sb[:, :, :], toks).then_inc(in_rest, 16)
            sp.dma_start(ctx_sb[:, :, :, :], ctx_tok).then_inc(in_rest, 16)
            sp.dma_start(probs_sb[:, :, :, :], probs).then_inc(in_rest, 16)
            sp.dma_start(mask_sb[:, :, :], mask).then_inc(in_rest, 16)
            sp.dma_start(tri_sb[:, :], tri).then_inc(in_rest, 16)

            for item in SCHED:
                kind = item[0]
                if kind == "qstore":
                    u = item[1]
                    chained(sp, ("qsplit", u))
                    sp.dma_start(q_dram[u], qp[UNITS[u][1]][:, :, :]).then_inc(q_stored[u], 16)
                elif kind == "kstore":
                    u = item[1]
                    n, i = KEYS[UNITS[u][0]], KSPLITS.index(u)
                    sp.wait_ge(keys_split, i + 1)
                    sp.dma_start(k_dram[u], kp[i % 2][:, :, 0:n]).then_inc(k_stored[u], 16)
                elif kind == "qload":
                    u = item[1]
                    layer, b = UNITS[u]
                    hd = head_dim(u)
                    sp.wait_ge(q_stored[u], 16)
                    if layer == SA0:
                        sp.wait_ge(packs_set, 6)
                    if layer == SA2:
                        sp.wait_ge(kones_set, 2)
                    for n in range(TERMS):
                        sp.dma_start(q_rows(u, n * hd, (n + 1) * hd)[:, 0:HEADS[layer] * T].rearrange("p (h t) -> p h t", t=T),
                                     q_dram[u][:, Q_TERM[n], :].rearrange("(h d) t -> d h t", d=hd)).then_inc(q_landed[u], 16)
                    if layer == CA3:
                        sp.dma_start(q_rows(u, MASK_ROW, MASK_ROW + 1), qones).then_inc(q_landed[u], 16)
                elif kind == "kload":
                    u = item[1]
                    layer, b = UNITS[u]
                    hd, n_keys = head_dim(u), KEYS[layer]
                    sp.wait_ge(k_stored[u], 16)
                    if layer in (SA0, CA1):
                        sp.wait_ge(packs_set, 6 if layer == SA0 else 8)
                    if layer == CA1 and b == 1:
                        sp.wait_ge(st_full, last_step(2 * SA0))
                    if layer == CA0:
                        sp.wait_ge(pool_step, POOL_SETUP)
                    if layer == SA2:
                        sp.wait_ge(kones_set, 2)
                    if layer == CA2:
                        sp.wait_ge(st_full, last_step(2 * CA0 + b))
                    if layer == CA3:
                        sp.wait_ge(kones_set, 4)
                        sp.wait_ge(mask_done, 2)
                        if b == 1:
                            sp.wait_ge(st_full, last_step(2 * SA2 + 1))
                    for n in range(TERMS):
                        sp.dma_start(k_rows(u, n * hd, (n + 1) * hd)[:, 0:HEADS[layer] * n_keys].rearrange("p (h t) -> p h t", t=n_keys),
                                     k_dram[u][:, K_TERM[n], :].rearrange("(h d) t -> d h t", d=hd)).then_inc(k_landed[u], 16)
                    if layer == CA3:
                        sp.dma_start(k_rows(u, MASK_ROW, MASK_ROW + 1).rearrange("p (h t) -> p h t", t=n_keys),
                                     mrow[:, b, :].unsqueeze(1).broadcast_to([1, 16, n_keys])).then_inc(k_landed[u], 16)
                elif kind == "shift":
                    gi = item[1]
                    u, g = GROUPS[gi]
                    at = TERM_ROWS
                    taken(sp, item)
                    for part in range(2):
                        sp.dma_start(q_rows(u, at + part, at + part + 1)[:, 4 * g * T:4 * (g + 1) * T],
                                     shift_t[gi % 4][4 * part:4 * part + 4, :]).then_inc(shift_landed[gi % 4], 16)
                elif kind == "zstore":
                    u = item[1]
                    b = UNITS[u][1]
                    taken(sp, ("finish", GROUP_AT[(u, 3)]))
                    for qt in range(QT):
                        sp.dma_start(z_dram[u][:, qt * 128:(qt + 1) * 128, :].rearrange("h s d -> s h d"),
                                     attn[b][:, qt, :].rearrange("p (h d) -> p h d", d=8)).then_inc(z_stored[u], 16)
                elif kind == "zload":
                    u = item[1]
                    b = UNITS[u][1]
                    sp.wait_ge(z_stored[u], 32)
                    sp.dma_start(z[b][:, :, :], z_dram[u].rearrange("(t h) (a r) d -> (h a) t (r d)", t=QT, r=16)).then_inc(z_landed[u], 16)
                elif kind == "outstore":
                    u = item[1]
                    b = UNITS[u][1]
                    chained(sp, ("outmul", u))
                    sp.dma_start(out[b].rearrange("(t p) d -> p t d", p=128), nrm[b][:, :, :]).then_inc(out_landed, 16)
            sp.wait_ge(out_landed, 16 * B)

        @block.tensor
        def _(pe):
            pe.wait_ge(consts_set, 3)

            def bias_row(dst, name, start):
                pe.matmul(dst, ones_row[:, 0:dst.shape[0]], row_sb[:, ROW[name], :], start=start, stop=False)

            def turn(key, src):
                dst = claim(pe, key)
                for qt in range(QT):
                    last = nc.tensor.transpose(dst[:, qt * 128:(qt + 1) * 128], src[:, qt, :], id_sb[:, :])
                last.then_inc(full(key), 1)

            def scores(gi, i):
                u, g = GROUPS[gi]
                layer, b = UNITS[u]
                qt, j0, n = tiles(gi)[i]
                rows_n, n_keys = TERM_ROWS, KEYS[layer]
                if g == 0 and i == 0:
                    pe.wait_ge(q_landed[u], 16 * (TERMS + (layer == CA3)))
                    pe.wait_ge(k_landed[u], 16 * (TERMS + (layer == CA3)))
                    if layer == SA0:
                        pe.wait_ge(in_const, 48)
                dst = claim(pe, ("scores", gi, i))
                for j in range(n):
                    h = 4 * g + j0 + j
                    to = dst[:, j * n_keys:(j + 1) * n_keys]
                    last = nc.tensor.matmul(to, q_rows(u, 0, rows_n)[:, h * T + qt * 128:h * T + (qt + 1) * 128],
                                            k_rows(u, 0, rows_n)[:, h * n_keys:(h + 1) * n_keys], start=True, stop=(layer != SA0))
                    if layer == SA0:
                        for p in SLOPE_OF[h]:
                            last = nc.tensor.matmul(to, slope_sb[:, p, :], dist_sb[:, qt, :], start=False, stop=(p == SLOPE_OF[h][-1]))
                last.then_inc(full(("scores", gi, i)), 1)

            def shift(gi):
                dst = claim(pe, ("shift", gi))
                pe.wait_ge(shift_ready, gi + 1)
                for qt in range(QT):
                    last = nc.tensor.transpose(dst[0:8, qt * 64:(qt + 1) * 64].bitcast(BF16),
                                               shift_p[gi % 2][:, qt, :, :].rearrange("p a h -> p (a h)"), idb_sb[:, :])
                last.then_inc(full(("shift", gi)), 1)

            def step(n):
                gi, kt = STEPS[n]
                u, g = GROUPS[gi]
                layer, b = UNITS[u]
                rows_n, n_keys = 128, KEYS[layer]
                if kt == 0:
                    pe.wait_ge(shift_landed[gi % 4], 32 * (gi // 4 + 1))
                if n >= 2:
                    pe.wait_ge(exp_done, n - 1)
                dst = st_ps[n % 2]
                for j in range(4):
                    h = 4 * g + j
                    to = dst[:, j * T:(j + 1) * T]
                    last = nc.tensor.matmul(to, k_rows(u, 0, rows_n)[:, h * n_keys + kt * 128:h * n_keys + (kt + 1) * 128],
                                            q_rows(u, 0, rows_n)[:, h * T:(h + 1) * T], start=True, stop=(layer != SA0))
                    if layer == SA0:
                        for p in SLOPE_OF[h]:
                            last = nc.tensor.matmul(to, slope_sb[:, p, :], dist_sb[:, kt, :], start=False, stop=(p == SLOPE_OF[h][-1]))
                last.then_inc(st_full, 1)

            def values(n):
                gi, kt = STEPS[n]
                u, g = GROUPS[gi]
                layer, b = UNITS[u]
                v = v_pack(u)
                wide = v.shape[3]
                last_kt = KEYS[layer] // 128 - 1
                pe.wait_ge(exp_done, n + 1)
                if kt == 0:
                    if g == 0:
                        taken(pe, ("vproj", u))
                        if layer == SA2:
                            pe.wait_ge(ones_cleared, b + 1)
                    if gi:
                        pe.wait_ge(o_taken, gi)
                e = probs_e[n % 3]
                if layer == SA2:
                    for j in range(4):
                        to = o_ps[32 * j:32 * j + wide, 0:T]
                        nc.tensor.matmul(to, den_sb[:, :], e[:, j * T:(j + 1) * T], start=(kt == 0), stop=False, skip_group_check=True)
                    if kt == 1:
                        for j in range(4):
                            nc.tensor.matmul(o_ps[32 * j:32 * j + wide, 0:128], v[:, kt, 4 * g + j, :], e[:, j * T:j * T + 128],
                                             start=False, stop=False, skip_group_check=True)
                    pe.wait_ge(masked, MASKED_AT[n] + 1)
                    for j in range(4):
                        last = nc.tensor.matmul(o_ps[32 * j:32 * j + wide, kt * 128:(kt + 1) * 128], v[:, kt, 4 * g + j, :],
                                                probs_m[n % 2][:, j, :], start=False, stop=(kt == last_kt), skip_group_check=True)
                else:
                    for j in range(4):
                        last = nc.tensor.matmul(o_ps[32 * j:32 * j + wide, 0:T], v[:, kt, 4 * g + j, :], e[:, j * T:(j + 1) * T],
                                                start=(kt == 0), stop=(kt == last_kt), skip_group_check=True)
                last.then_inc(values_done, 1)

            def scan():
                for b in range(B):
                    taken(pe, ("uproj", 2 * CA1 + b))
                pe.wait_ge(exp_done, last_step(2 * CA1 + 1))
                nc.tensor.matmul(scan_ps, W("at", S_STATE), UT[:, :, :].rearrange("p t b -> p (t b)"),
                                 start=True, stop=False, skip_group_check=True).then_inc(scan_pre, 1)
                for t in range(2, T):
                    pe.wait_ge(scan_g, t - 1)
                    nc.tensor.matmul(scan_ps[:, (t - 1) * B:t * B], W("at", S_STATE), G[:, t - 1, :], start=False,
                                     stop=(t == T - 1), skip_group_check=True).then_inc(scan_h, 1)

            for item in SCHED:
                kind = item[0]
                if kind == "scores":
                    scores(item[1], item[2])
                elif kind == "shift":
                    shift(item[1])
                elif kind == "step":
                    step(item[1])
                elif kind == "values":
                    values(item[1])
                elif kind == "finish":
                    gi = item[1]
                    dst = claim(pe, item)
                    pe.wait_ge(o_taken, gi + 1)
                    for qt in range(QT):
                        last = nc.tensor.transpose(dst[:, qt * 128:(qt + 1) * 128], o_sb[gi % 2][:, qt * 128:(qt + 1) * 128], id_sb[:, :])
                    last.then_inc(full(item), 1)
                elif kind == "attnT":
                    u = item[1]
                    taken(pe, ("finish", GROUP_AT[(u, HEADS[UNITS[u][0]] // 4 - 1)]))
                    turn(item, attn[UNITS[u][1]])
                elif kind == "oproj":
                    u = item[1]
                    layer, b = UNITS[u]
                    taken(pe, ("attnT", u))
                    pe.wait_ge(in_rest, 128)
                    dst = claim(pe, item)
                    for qt in range(QT):
                        to = dst[:, qt * 128:(qt + 1) * 128]
                        if layer != CA3:
                            bias_row(to, f"bo{layer}", True)
                        last = nc.tensor.matmul(to, attnT[b][:, qt * 128:(qt + 1) * 128], W(f"o{layer}"), start=(layer == CA3), stop=True)
                    last.then_inc(full(item), 1)
                elif kind == "nT":
                    chained(pe, ("norm", item[1], item[2]))
                    turn(item, nrm[UNITS[item[1]][1]])
                elif kind == "xT":
                    taken(pe, ("ssm", item[1]))
                    turn(item, X[item[1]])
                elif kind == "cT":
                    pe.wait_ge(cn_done, CNORMS.index(item[1]) + 1)
                    dst = claim(pe, item)
                    for kt in range(4):
                        last = nc.tensor.transpose(dst[:, kt * 128:(kt + 1) * 128], cn[:, kt, :], id_sb[:, :])
                    last.then_inc(full(item), 1)
                elif kind in ("qproj", "kproj"):
                    u = item[1]
                    layer, b = UNITS[u]
                    if kind == "qproj":
                        source_ready(pe, u)
                        src = query_source(u)
                    else:
                        src = key_source(pe, u)
                    if layer != SA0:
                        pe.wait_ge(in_rest, 128)
                    dst = claim(pe, item)
                    nc.tensor.matmul(dst[:, 0:src.shape[1]], W(f"{kind[0]}{layer}"), src, start=True, stop=True).then_inc(full(item), 1)
                elif kind == "vproj":
                    u = item[1]
                    layer = UNITS[u][0]
                    src = key_source(pe, u)
                    dst = claim(pe, item)
                    for kt in range(KEYS[layer] // 128):
                        to = dst[:, kt * 128:(kt + 1) * 128]
                        if layer != CA3:
                            bias_row(to, f"bv{layer}", True)
                        last = nc.tensor.matmul(to, src[:, kt * 128:(kt + 1) * 128], W(f"v{layer}"), start=(layer == CA3), stop=True)
                    last.then_inc(full(item), 1)
                elif kind == "glu":
                    u, f = item[1], item[2]
                    b = UNITS[u][1]
                    taken(pe, ("nT", u, "a"))
                    dst = claim(pe, item)
                    for i in range(2):
                        at = i * F_FF + f * 128
                        last = nc.tensor.matmul(dst[:, i * T:(i + 1) * T], W("w12")[:, at:at + 128], XT[b][:, :], start=True, stop=True)
                    last.then_inc(full(item), 1)
                elif kind == "relu":
                    u = item[1]
                    taken(pe, ("nT", u, "a"))
                    dst = claim(pe, item)
                    nc.tensor.matmul(dst[:, 0:T], W("f1"), XT[UNITS[u][1]][:, :], start=True, stop=True).then_inc(full(item), 1)
                elif kind == "ffout":
                    u = item[1]
                    layer, b = UNITS[u]
                    glu = layer == CA0
                    taken(pe, ("glu", u, 3) if glu else ("relu", u))
                    dst = claim(pe, item)
                    for qt in range(QT):
                        to = dst[:, qt * 128:(qt + 1) * 128]
                        bias_row(to, "b3" if glu else "bf2", True)
                        for f in range(4 if glu else 1):
                            rhs = W("w3")[:, f * 128:(f + 1) * 128] if glu else W("f2")
                            last = nc.tensor.matmul(to, hT[:, f, qt * 128:(qt + 1) * 128], rhs, start=False, stop=(f == (3 if glu else 0)))
                    last.then_inc(full(item), 1)
                elif kind == "win":
                    u = item[1]
                    taken(pe, ("nT", u, "a"))
                    dst = claim(pe, item)
                    nc.tensor.matmul(dst[:, 0:T], W("win"), XT[UNITS[u][1]][:, :], start=True, stop=True).then_inc(full(item), 1)
                elif kind == "uproj":
                    u = item[1]
                    taken(pe, ("win", u))
                    dst = claim(pe, item)
                    nc.tensor.matmul(dst[0:S_STATE, 0:T], W("bmat"), hT[:, 0, :], start=True, stop=True).then_inc(full(item), 1)
                elif kind == "scan":
                    scan()
                elif kind == "ssm":
                    b = item[1]
                    pe.wait_ge(states_done, 1)
                    dst = claim(pe, item)
                    for qt in range(QT):
                        to = dst[:, qt * 128:(qt + 1) * 128]
                        nc.tensor.matmul(to, ones_row[:, :], modrow[:, b, :], start=True, stop=False)
                        last = nc.tensor.matmul(to, G[:, qt * 128:(qt + 1) * 128, b], W("cmat", S_STATE), start=False, stop=True)
                    last.then_inc(full(item), 1)
                elif kind == "mod1":
                    pe.wait_ge(in_rest, 128)
                    dst = claim(pe, item)
                    for b in range(B):
                        for kt in range(4):
                            last = nc.tensor.matmul(dst[0:P_PROG, b:b + 1], probs_sb[:, b, kt, :], inv_col[:, :], start=(kt == 0), stop=(kt == 3))
                    last.then_inc(full(item), 1)
                elif kind == "mod2":
                    taken(pe, ("mod1",))
                    dst = claim(pe, item)
                    for b in range(B):
                        to = dst[0:1, b * 128:(b + 1) * 128]
                        bias_row(to, "bprog", True)
                        last = nc.tensor.matmul(to, pmean[:, b:b + 1], W("prog", P_PROG), start=False, stop=True)
                    last.then_inc(full(item), 1)
                elif kind == "flag":
                    pe.wait_ge(mask_done, 2)
                    dst = claim(pe, item)
                    nc.tensor.matmul(dst[:, 0:B], ones_row[:, :], flag_row[:, :], start=True, stop=True).then_inc(full(item), 1)

        @block.scalar
        def _(act):
            act.wait_ge(in_first, 64)

            for item in SCHED:
                kind = item[0]
                if kind == "step":
                    n = item[1]
                    act.wait_ge(st_full, n + 1)
                    if n >= 3:
                        act.wait_ge(values_done, n - 2)
                    nc.scalar.activation(probs_e[n % 3][:, :], st_ps[n % 2][:, :], ACT.Exp).then_inc(exp_done, 1)
                elif kind == "finish":
                    gi = item[1]
                    act.wait_ge(values_done, STEP_AT[(gi, KEYS[UNITS[GROUPS[gi][0]][0]] // 128 - 1)] + 1)
                    if gi >= 2:
                        filled(act, ("finish", gi - 2))
                    nc.scalar.activation(o_sb[gi % 2][:, :], o_ps[:, 0:T], ACT.Copy).then_inc(o_taken, 1)
                elif kind == "shift":
                    gi = item[1]
                    src = filled(act, item)
                    if gi >= 4:
                        act.wait_ge(shift_landed[gi % 4], 32 * (gi // 4))
                    nc.scalar.activation(shift_t[gi % 4][:, :], src[0:8, 0:T // 2].bitcast(BF16), ACT.Copy).then_inc(free(item), 1)
                elif kind == "attnT":
                    src = filled(act, item)
                    nc.scalar.activation(attnT[UNITS[item[1]][1]][:, :], src[:, 0:T], ACT.Copy).then_inc(free(item), 1)
                elif kind == "nT":
                    u, tag = item[1], item[2]
                    layer, b = UNITS[u]
                    g, bias = NORM_COLS[(layer, tag)]
                    src = filled(act, item)
                    nc.scalar.activation(XT[b][:, :], src[:, 0:T], ACT.Identity, scale=C(g), bias=C(bias) if bias else 0.0).then_inc(free(item), 1)
                elif kind == "xT":
                    src = filled(act, item)
                    nc.scalar.activation(XT[item[1]][:, :], src[:, 0:T], ACT.Copy).then_inc(free(item), 1)
                elif kind == "cT":
                    u = item[1]
                    layer, b = UNITS[u]
                    src = filled(act, item)
                    nc.scalar.activation(cT[:, :], src[:, :], ACT.Identity, scale=C("g_x1" if layer == CA1 else "g_c"),
                                         bias=C("b_x1") if layer == CA1 else 0.0).then_inc(free(item), 1)
                elif kind == "kproj":
                    u = item[1]
                    layer = UNITS[u][0]
                    n, i = KEYS[layer], KSPLITS.index(u)
                    src = filled(act, item)
                    if i >= 1:
                        act.wait_ge(keys_split, i)
                    nc.scalar.activation(kf[:, 0:n], src[:, 0:n], ACT.Identity, bias=C(f"bk{layer}") if layer != CA3 else 0.0)\
                        .then_inc(free(item), 1)
                elif kind == "vproj":
                    u = item[1]
                    layer, b = UNITS[u]
                    hd, nkt = head_dim(u), KEYS[layer] // 128
                    src = filled(act, item)
                    act.wait_ge(consts_set, 3)
                    act.wait_ge(pool_step, POOL_SETUP)
                    if layer >= SA2:
                        act.wait_ge(values_done, last_step({SA2: 2 * SA0, CA2: 2 * CA0, CA3: 2 * CA1}[layer] + b))
                    if layer == CA3:
                        act.wait_ge(kones_set, 4)
                        taken(act, ("flag",))
                    nc.scalar.activation(v_pack(u)[:, :, :, 0:hd], src[:, 0:nkt * 128].rearrange("p (t h d) -> p t h d", t=nkt, d=hd),
                                         ACT.Copy, scale=flag[:, b:b + 1] if layer == CA3 else 1.0).then_inc(free(item), 1)
                elif kind == "glu":
                    u, f = item[1], item[2]
                    b = UNITS[u][1]
                    src = filled(act, item)
                    if f:
                        taken(act, ("glu", u, f - 1))
                    nc.scalar.activation(glu_t[b][:, :], src[:, 0:T], ACT.Tanh, scale=0.5, bias=half_b[:, f:f + 1]).then_inc(gate_done, 1)
                elif kind == "relu":
                    src = filled(act, item)
                    nc.scalar.activation(hT[:, 0, :], src[:, 0:T], ACT.Relu, bias=C("b_f1")).then_inc(free(item), 1)
                elif kind == "win":
                    src = filled(act, item)
                    nc.scalar.activation(hT[:, 0, :], src[:, 0:T], ACT.Identity, bias=C("b_in")).then_inc(free(item), 1)
                elif kind == "uproj":
                    src = filled(act, item)
                    nc.scalar.activation(UT[:, :, UNITS[item[1]][1]], src[0:S_STATE, 0:T], ACT.Copy).then_inc(free(item), 1)
                elif kind == "scan":
                    act.wait_ge(scan_pre, 1)
                    for t in range(1, T):
                        if t >= 2:
                            act.wait_ge(scan_h, t - 1)
                        nc.scalar.activation(G[:, t, :], scan_ps[:, (t - 1) * B:t * B], ACT.Silu).then_inc(scan_g, 1)
                elif kind == "mod1":
                    src = filled(act, item)
                    nc.scalar.activation(pmean[:, :], src[0:P_PROG, 0:B], ACT.Copy).then_inc(free(item), 1)
                elif kind == "mod2":
                    src = filled(act, item)
                    nc.scalar.activation(modrow[:, :, :], src[0:1, 0:B * 128].rearrange("p (b d) -> p b d", b=B), ACT.Copy).then_inc(free(item), 1)
                elif kind == "flag":
                    src = filled(act, item)
                    nc.scalar.activation(flag[:, :], src[:, 0:B], ACT.Copy).then_inc(free(item), 1)

        @block.vector
        def _(dve):
            steps = [0]

            def own(ins):
                steps[0] += 1
                ins.then_inc(dve_step, 1)

            def after_own():
                dve.wait_ge(dve_step, steps[0])

            for b in range(B):
                for lo, hi in ((32, 64), (64, 128)):
                    nc.vector.memset(q_pack[b][lo:hi, :].bitcast(F32), 0.0).then_inc(packs_set, 1)
            own(nc.vector.memset(k_odd[1][64:128, :].bitcast(F32), 0.0))
            nc.vector.memset(k_odd[1][32:64, :].bitcast(F32), 0.0).then_inc(packs_set, 1)
            after_own()
            nc.vector.memset(k_odd[1][TERM_ROWS:TERM_ROWS + 2, :], 1.0).then_inc(packs_set, 1)
            own(nc.vector.memset(k_odd[0][96:128, 0:8 * S2].bitcast(F32), 0.0))
            after_own()
            nc.vector.memset(k_odd[0][TERM_ROWS:TERM_ROWS + 2, 0:8 * S2], 1.0).then_inc(packs_set, 2)
            nc.vector.memset(ones_row[:, :], 1.0)
            nc.vector.memset(inv_col[:, :], 1.0 / S2)
            nc.vector.memset(o_ps[:, :], 0.0).then_inc(consts_set, 1)
            own(nc.vector.memset(den_sb[:, :], 0.0))
            after_own()
            nc.vector.memset(den_sb[:, 8:9], 1.0).then_inc(consts_set, 1)
            dve.wait_ge(in_first, 64)
            nc.vector.tensor_scalar(half_b[:, :], col_sb[:, COL["b12_0"]:COL["b12_0"] + 4], 0.5, None, ALU.mult).then_inc(consts_set, 1)
            dve.wait_ge(in_const, 48)
            nc.vector.tensor_copy(idb_sb[:, :], id_sb[:, :]).then_inc(idb_done, 1)

            def residual(u):
                b = UNITS[u][1]
                done = [SIDE[i] for i in SCHED[:SCHED.index(("oproj", u) if ("oproj", u) in BANK else ("zadd", u))] if i[0] == "tok" and UNITS[i[1]][1] == b]
                if done:
                    dve.wait_ge(side_s[b], max(done))
                else:
                    dve.wait_ge(in_rest, 128)

            for item in SCHED:
                kind = item[0]
                if kind == "scores":
                    gi, i = item[1], item[2]
                    qt, j0, n = tiles(gi)[i]
                    src = filled(dve, item)
                    nc.vector.tensor_reduce(rowmax[gi % 2][:, qt, j0:j0 + n], src[:, :].rearrange("p (h k) -> p h k", h=n), AX_X, ALU.max)\
                        .then_inc(free(item), 1)
                    if i == len(tiles(gi)) - 1:
                        for t in range(max(0, i - RING + 1), i + 1):
                            taken(dve, ("scores", gi, t))
                        if gi >= 2:
                            filled(dve, ("shift", gi - 2))
                        own(nc.vector.tensor_scalar(shift_p[gi % 2][:, :, 0, :], rowmax[gi % 2][:, :, :], -1.0, None, ALU.mult))
                        after_own()
                        nc.vector.scalar_tensor_tensor(shift_p[gi % 2][:, :, 1, :], rowmax[gi % 2][:, :, :], -1.0,
                                                       shift_p[gi % 2][:, :, 0, :], ALU.mult, ALU.subtract).then_inc(shift_ready, 1)
                elif kind == "finish":
                    gi = item[1]
                    u, g = GROUPS[gi]
                    b, hd = UNITS[u][1], head_dim(u)
                    src = filled(dve, item)[:, 0:T].rearrange("p (t j c) -> p t j c", t=QT, j=4)
                    if gi:
                        taken(dve, ("finish", gi - 1))
                    own(nc.vector.reciprocal(rden[:, :, :, :], src[:, :, :, hd:hd + 1]))
                    after_own()
                    for qt in range(QT):
                        last = nc.vector.tensor_tensor(attn[b][:, qt, 4 * g * hd:4 * (g + 1) * hd].rearrange("p (j d) -> p j d", j=4),
                                                       src[:, qt, :, 0:hd], rden[:, qt, :, :].broadcast_to([128, 4, hd]), ALU.mult)
                    last.then_inc(free(item), 1)
                elif kind in ("oproj", "ffout"):
                    u = item[1]
                    layer, b = UNITS[u]
                    src = filled(dve, item)
                    if kind == "ffout":
                        dve.wait_ge(side_s[b], SIDE[("tok", u, "a")])
                    else:
                        residual(u)
                    to = X[b] if layer == CA1 else r[b]
                    nc.vector.tensor_tensor(to[:, :, :], src[:, 0:T].rearrange("p (t d) -> p t d", t=QT), X[b][:, :, :], ALU.add).then_inc(free(item), 1)
                elif kind == "zadd":
                    u = item[1]
                    b = UNITS[u][1]
                    residual(u)
                    dve.wait_ge(z_landed[u], 16)
                    nc.vector.tensor_tensor(r[b][:, :, :], z[b][:, :, :], X[b][:, :, :], ALU.add).then_inc(chain_s[b], 1)
                elif kind == "ssm":
                    b = item[1]
                    src = filled(dve, item)
                    nc.vector.tensor_tensor(X[b][:, :, :], src[:, 0:T].rearrange("p (t d) -> p t d", t=QT), X[b][:, :, :], ALU.add).then_inc(free(item), 1)
                elif kind == "stats":
                    u, tag = item[1], item[2]
                    layer, b = UNITS[u]
                    rms, src = (layer, tag) in RMS, X[b] if (layer, tag) in FROM_X else r[b]
                    if tag == "c":
                        chained(dve, ("tokd", u, "b"))
                    elif tag == "b":
                        taken(dve, ("ffout", u))
                    elif layer in (SA2, CA2):
                        chained(dve, ("zadd", u))
                    else:
                        taken(dve, ("oproj", u))
                    for qt in range(QT):
                        own(nc.vector.bn_stats(stats[b][:, qt, :], src[:, qt, :]))
                    after_own()
                    for qt in range(QT):
                        own(nc.vector.bn_aggr(mv[b][:, qt, :], stats[b][:, qt, :]))
                    after_own()
                    if rms:
                        own(nc.vector.tensor_tensor(ve[b][:, :], mv[b][:, :, 0], mv[b][:, :, 0], ALU.mult))
                        after_own()
                        nc.vector.scalar_tensor_tensor(ve[b][:, :], mv[b][:, :, 1], EPS[True], ve[b][:, :], ALU.add, ALU.add).then_inc(chain_s[b], 1)
                    else:
                        nc.vector.tensor_scalar(ve[b][:, :], mv[b][:, :, 1], EPS[False], None, ALU.add).then_inc(chain_s[b], 1)
                elif kind == "norm":
                    u, tag = item[1], item[2]
                    layer, b = UNITS[u]
                    rms, src = (layer, tag) in RMS, X[b] if (layer, tag) in FROM_X else r[b]
                    chained(dve, ("pow", u, tag))
                    for qt in range(QT):
                        if rms:
                            last = nc.vector.tensor_scalar(nrm[b][:, qt, :], src[:, qt, :], rs[b][:, qt:qt + 1], None, ALU.mult)
                        else:
                            last = nc.vector.tensor_scalar(nrm[b][:, qt, :], src[:, qt, :], mv[b][:, qt, 0:1], rs[b][:, qt:qt + 1], ALU.subtract, ALU.mult)
                    last.then_inc(chain_s[b], 1)
                elif kind == "tokd":
                    u, tag = item[1], item[2]
                    layer, b = UNITS[u]
                    g, bias = NORM_TOKS[(layer, tag)]
                    chained(dve, ("norm", u, tag))
                    own(nc.vector.tensor_tensor(r[b][:, :, :], nrm[b][:, :, :], tok_sb[:, TOK[g]:TOK[g] + 1, :].broadcast_to([128, QT, D]), ALU.mult))
                    after_own()
                    nc.vector.tensor_tensor(X[b][:, :, :], r[b][:, :, :], tok_sb[:, TOK[bias]:TOK[bias] + 1, :].broadcast_to([128, QT, D]), ALU.add)\
                        .then_inc(chain_s[b], 1)
                elif kind == "outmul":
                    u = item[1]
                    b = UNITS[u][1]
                    chained(dve, ("norm", u, "a"))
                    nc.vector.tensor_tensor(nrm[b][:, :, :], nrm[b][:, :, :], tok_sb[:, TOK["g_out"]:TOK["g_out"] + 1, :].broadcast_to([128, QT, D]), ALU.mult)\
                        .then_inc(chain_s[b], 1)
                elif kind == "qproj":
                    u = item[1]
                    layer, b = UNITS[u]
                    dve.wait_ge(in_first, 64)
                    if u >= 2:
                        dve.wait_ge(q_stored[u - 2], 16)
                    src = filled(dve, item)
                    nc.vector.tensor_scalar(qf[b][:, :], src[:, 0:T], C(f"bq{layer}") if layer != CA3 else 0.0, SCALE[layer], ALU.add, ALU.mult).then_inc(free(item), 1)
                elif kind == "qsplit":
                    u = item[1]
                    b = UNITS[u][1]
                    taken(dve, ("qproj", u))
                    own(nc.vector.tensor_copy(qp[b][:, 0, :], qf[b][:, :]))
                    after_own()
                    own(nc.vector.tensor_tensor(qr[b][:, :], qf[b][:, :], qp[b][:, 0, :], ALU.subtract))
                    after_own()
                    own(nc.vector.tensor_copy(qp[b][:, 1, :], qr[b][:, :]))
                    after_own()
                    nc.vector.tensor_tensor(qp[b][:, 2, :], qr[b][:, :], qp[b][:, 1, :], ALU.subtract).then_inc(chain_s[b], 1)
                elif kind == "glu":
                    u, f = item[1], item[2]
                    b = UNITS[u][1]
                    dve.wait_ge(gate_done, GLUS.index(item) + 1)
                    src = filled(dve, item)
                    own(nc.vector.tensor_scalar(glu_a[b][:, :], src[:, 0:T], C(f"b12_{f}"), 0.5, ALU.add, ALU.mult))
                    after_own()
                    own(nc.vector.scalar_tensor_tensor(glu_w[b][:, :], glu_t[b][:, :], 1.0, glu_a[b][:, :], ALU.add, ALU.mult))
                    after_own()
                    nc.vector.scalar_tensor_tensor(hT[:, f, :], src[:, T:2 * T], C(f"b12_{f + 4}"), glu_w[b][:, :], ALU.add, ALU.mult).then_inc(free(item), 1)
                elif kind == "ctxstats":
                    dve.wait_ge(in_rest, 128)
                    for i in range(8):
                        own(nc.vector.bn_stats(cstats[:, i, :], ctx_sb[:, i // 4, i % 4, :]))
                    after_own()
                    for i in range(8):
                        own(nc.vector.bn_aggr(cmv[:, i, :], cstats[:, i, :]))
                    after_own()
                    own(nc.vector.tensor_tensor(cve[:, 1, :], cmv[:, :, 0], cmv[:, :, 0], ALU.mult))
                    after_own()
                    own(nc.vector.scalar_tensor_tensor(cve[:, 1, :], cmv[:, :, 1], EPS[True], cve[:, 1, :], ALU.add, ALU.add))
                    after_own()
                    nc.vector.tensor_scalar(cve[:, 0, :], cmv[:, :, 1], EPS[False], None, ALU.add).then_inc(cstats_done, 1)
                elif kind == "maskprep":
                    own(nc.vector.tensor_scalar(mrow, mask_sb[:, :, :], -1.0, BIG, ALU.add, ALU.mult))
                    after_own()
                    nc.vector.tensor_reduce(flag_row[:, :], mask_sb[:, :, :], AX_X, ALU.max).then_inc(mask_done, 2)
                elif kind == "scan":
                    for b in range(B):
                        taken(dve, ("uproj", 2 * CA1 + b))
                    own(nc.vector.memset(G[:, 0, :], 0.0))
                    after_own()
                    dve.wait_ge(scan_g, T - 1)
                    nc.vector.tensor_tensor(G[:, :, :], G[:, :, :], UT[:, :, :], ALU.add).then_inc(states_done, 1)

        @block.gpsimd
        def _(pool):
            steps = [0]

            def own(ins):
                steps[0] += 1
                ins.then_inc(pool_step, 1)
                pool.wait_ge(pool_step, steps[0])

            own(nc.gpsimd.memset(half[:, :], -0.5))
            for tensors, heads, wide, at in ((v_self, 16, 16, 8), (v_even, 16, 16, 8), (v_odd, 8, 32, 16)):
                for b in range(B):
                    own(nc.gpsimd.memset(tensors[b][:, :], 0.0))
                    own(nc.gpsimd.memset(tensors[b][:, :].rearrange("p (t h c) -> p t h c", h=heads, c=wide)[:, :, :, at:at + 1], 1.0))
            for b in range(B):
                own(nc.gpsimd.memset(k_even[b][32:64, :].bitcast(F32), 0.0))
                own(nc.gpsimd.memset(k_even[b][64:128, :].bitcast(F32), 0.0))
                own(nc.gpsimd.memset(k_even[b][TERM_ROWS:TERM_ROWS + 2, :], 1.0))
            assert steps[0] == POOL_SETUP

            for item in SCHED:
                kind = item[0]
                if kind == "pow":
                    u, tag = item[1], item[2]
                    b = UNITS[u][1]
                    chained(pool, ("stats", u, tag))
                    nc.gpsimd.tensor_tensor(rs[b][:, :], ve[b][:, :], half[:, 0:QT], ALU.pow).then_inc(chain_s[b], 1)
                    chained(pool, item)
                elif kind == "tok":
                    u, tag = item[1], item[2]
                    layer, b = UNITS[u]
                    g, bias = NORM_TOKS[(layer, tag)]
                    chained(pool, ("norm", u, tag))
                    own(nc.gpsimd.tensor_tensor(X[b][:, :, :], nrm[b][:, :, :], tok_sb[:, TOK[g]:TOK[g] + 1, :].broadcast_to([128, QT, D]), ALU.mult))
                    nc.gpsimd.tensor_tensor(X[b][:, :, :], X[b][:, :, :], tok_sb[:, TOK[bias]:TOK[bias] + 1, :].broadcast_to([128, QT, D]), ALU.add)\
                        .then_inc(side_s[b], 1)
                    pool.wait_ge(side_s[b], SIDE[item])
                elif kind == "ksplit":
                    u = item[1]
                    n, i = KEYS[UNITS[u][0]], KSPLITS.index(u)
                    f, p = kf, kp[i % 2]
                    taken(pool, ("kproj", u))
                    if i >= 2:
                        pool.wait_ge(k_stored[KSPLITS[i - 2]], 16)
                    own(nc.gpsimd.tensor_copy(p[:, 0, 0:n], f[:, 0:n]))
                    own(nc.gpsimd.tensor_tensor(f[:, 0:n], f[:, 0:n], p[:, 0, 0:n], ALU.subtract))
                    own(nc.gpsimd.tensor_copy(p[:, 1, 0:n], f[:, 0:n]))
                    nc.gpsimd.tensor_tensor(p[:, 2, 0:n], f[:, 0:n], p[:, 1, 0:n], ALU.subtract).then_inc(keys_split, 1)
                    pool.wait_ge(keys_split, i + 1)
                elif kind == "values":
                    n = item[1]
                    gi, kt = STEPS[n]
                    if UNITS[GROUPS[gi][0]][0] == SA2:
                        pool.wait_ge(exp_done, n + 1)
                        pool.wait_ge(values_done, n - 1)
                        src = probs_e[n % 3][:, :].rearrange("p (j t) -> p j t", j=4)[:, :, kt * 128:(kt + 1) * 128]
                        nc.gpsimd.tensor_tensor(probs_m[n % 2][:, :, :], src, tri_sb[:, :].unsqueeze(1).broadcast_to([128, 4, 128]), ALU.mult).then_inc(masked, 1)
                        pool.wait_ge(masked, MASKED_AT[n] + 1)
                elif kind == "ctxstats":
                    pool.wait_ge(cstats_done, 1)
                    for i in range(2):
                        nc.gpsimd.tensor_tensor(crs[:, i, :], cve[:, i, :], half[:, :], ALU.pow).then_inc(crs_done, 1)
                        pool.wait_ge(crs_done, i + 1)
                elif kind == "cnorm":
                    u = item[1]
                    layer, b = UNITS[u]
                    i = CNORMS.index(u)
                    pool.wait_ge(crs_done, 2)
                    if i:
                        k, n = BANK[("cT", CNORMS[i - 1])]
                        pool.wait_ge(bank_full[k], n + 1)
                    for kt in range(4):
                        t = 4 * b + kt
                        if layer == CA1:
                            last = nc.gpsimd.tensor_scalar(cn[:, kt, :], ctx_sb[:, b, kt, :], cmv[:, t, 0:1], crs[:, 0, t:t + 1], ALU.subtract, ALU.mult)
                        else:
                            last = nc.gpsimd.tensor_scalar(cn[:, kt, :], ctx_sb[:, b, kt, :], crs[:, 1, t:t + 1], None, ALU.mult)
                        if kt < 3:
                            own(last)
                    last.then_inc(cn_done, 1)
                    pool.wait_ge(cn_done, i + 1)
                elif kind == "mod1":
                    for b in range(B):
                        pool.wait_ge(values_done, last_step(2 * SA0 + b))
                        nc.gpsimd.memset(v_self[b][:, :].rearrange("p (t h c) -> p t h c", h=16, c=16)[:, :, :, 8:9], 0.0).then_inc(ones_cleared, 1)
                        pool.wait_ge(ones_cleared, b + 1)
                elif kind == "scan":
                    pool.wait_ge(st_full, last_step(2 * CA1 + 1))
                    for b in range(B):
                        own(nc.gpsimd.memset(q_pack[b][32:64, :].bitcast(F32), 0.0))
                        own(nc.gpsimd.memset(q_pack[b][64:96, :].bitcast(F32), 0.0))
                    own(nc.gpsimd.memset(k_odd[1][32:64, :].bitcast(F32), 0.0))
                    nc.gpsimd.memset(k_odd[1][64:96, :].bitcast(F32), 0.0).then_inc(kones_set, 2)
                    pool.wait_ge(kones_set, 2)
                    pool.wait_ge(values_done, last_step(2 * CA1 + 1))
                    for b in range(B):
                        own(nc.gpsimd.memset(v_odd[b][:, :], 0.0))
                        own(nc.gpsimd.memset(v_odd[b][:, :].rearrange("p (t h c) -> p t h c", h=16, c=16)[:, :, :, 8:9], 1.0))
                    own(nc.gpsimd.memset(k_odd[0][32:64, :].bitcast(F32), 0.0))
                    own(nc.gpsimd.memset(k_odd[0][64:128, :].bitcast(F32), 0.0))
                    nc.gpsimd.memset(k_odd[0][TERM_ROWS:TERM_ROWS + 2, :], 1.0).then_inc(kones_set, 2)
                    pool.wait_ge(kones_set, 4)



POOL_SETUP = 19
GLUS = [i for i in SCHED if i[0] == "glu"]
MASKED_AT = {n: i for i, n in enumerate(it[1] for it in SCHED if it[0] == "values" and UNITS[GROUPS[STEPS[it[1]][0]][0]][0] == SA2)}


def kernel(**inputs):
    import ml_dtypes
    import concourse.bacc as bacc
    from concourse.bass_utils import run_bass_kernel_spmd

    a = {k: np.asarray(v) for k, v in inputs.items()}
    L0, L1, L2, L3 = (lambda n, i=i: a[f"L{i}_xattn_{n}"] for i in range(4))
    f32 = np.float32

    def pad(m):
        return np.concatenate([m, np.zeros((128 - m.shape[0], m.shape[1]), m.dtype)], 0) if m.shape[0] < 128 else m

    qkv0, kv1, qkv2 = L0("qkv_w").T, L0("kv_w").T, L1("W_qkv").T
    w = {"q0": qkv0[:, 0:128], "k0": qkv0[:, 128:256], "v0": qkv0[:, 256:384], "o0": L0("self_out_w").T,
         "q1": L0("q_w").T, "k1": kv1[:, 0:128], "v1": kv1[:, 128:256], "o1": L0("cross_out_w").T, "w12": L0("w12").T,
         "w3": L0("w3").T.reshape(4, 128, 128).transpose(1, 0, 2).reshape(128, 512),
         "q2": qkv2[:, 0:128], "k2": qkv2[:, 128:256], "v2": qkv2[:, 256:384], "o2": L1("W_o").T, "win": L1("W_in").T,
         "bmat": L1("Bmat"), "at": L1("A").T, "cmat": L1("Cmat"), "prog": L1("W_prog").T,
         "q3": L2("sa_wq"), "k3": L2("sa_wk"), "v3": L2("sa_wv"), "q4": L2("ca_wq"), "k4": L2("ca_wk"), "v4": L2("ca_wv"),
         "f1": L2("ffn_w1"), "f2": L2("ffn_w2"), "q5": L3("Wq"), "k5": L3("Wk"), "v5": L3("Wv"), "o5": L3("Wo")}
    w = np.concatenate([pad(w[n]) for n in W_COLS], 1)
    b0, b2 = L0("qkv_b"), L1("b_qkv")
    col = {"bq0": b0[0:128], "bk0": b0[128:256], "bq1": L0("q_b"), "bk1": L0("kv_b")[0:128], "bq2": b2[0:128], "bk2": b2[128:256],
           "bq3": L2("sa_bq"), "bk3": L2("sa_bk"), "bq4": L2("ca_bq"), "bk4": L2("ca_bk"),
           "g_ln1": L0("ln1_g"), "b_ln1": L0("ln1_b"), "g_ln2": L0("ln2_g"), "b_ln2": L0("ln2_b"),
           "g_x1": L1("g1"), "b_x1": L1("beta1"), "g_x2": L1("g2"), "b_x2": L1("beta2"), "b_in": L1("b_in"),
           "g_sa": L2("sa_g"), "b_sa": L2("sa_b"), "g_ca": L2("ca_g"), "b_ca": L2("ca_b"), "b_f1": L2("ffn_b1"),
           "g_q": L3("g_q"), "g_c": L3("g_c")}
    col |= {f"b12_{i}": L0("b12")[i * 128:(i + 1) * 128] for i in range(8)}
    cols = np.stack([col[n] for n in COLS], 1)
    row = {"bv0": b0[256:384], "bo0": L0("self_out_b"), "bv1": L0("kv_b")[128:256], "bo1": L0("cross_out_b"), "b3": L0("b3"),
           "bv2": b2[256:384], "bo2": L1("b_o"), "bprog": L1("b_prog"), "bv3": L2("sa_bv"), "bv4": L2("ca_bv"), "bf2": L2("ffn_b2")}
    rows = np.stack([row[n] for n in ROWS], 0)[None]
    tok = {"g_ln1": L0("ln1_g"), "b_ln1": L0("ln1_b"), "g_ln2": L0("ln2_g"), "b_ln2": L0("ln2_b"), "g_ln3": L0("ln3_g"), "b_ln3": L0("ln3_b"),
           "g_sa": L2("sa_g"), "b_sa": L2("sa_b"), "g_ca": L2("ca_g"), "b_ca": L2("ca_b"), "g_ffn": L2("ffn_g"), "b_ffn": L2("ffn_b"),
           "g_out": L3("g_out")}
    toks = np.broadcast_to(np.stack([tok[n] for n in TOKS], 0)[None], (128, len(TOKS), 128))
    x, ctx = a["x"], a["ctx_1024"]
    i = np.arange(128)
    dist = -np.abs(np.arange(T)[:, None] - np.arange(T)[None, :]).reshape(2, 128, T).transpose(1, 0, 2)
    slopes = np.stack([np.eye(128) * p for _, p in SLOPE_PARTS], 1)
    arrays = {
        "in_x_tok": x.reshape(B, QT, 128, D).transpose(0, 2, 1, 3),
        "in_x_t": x.transpose(2, 0, 1),
        "in_ctx_tok": ctx.reshape(B, 4, 128, D).transpose(2, 0, 1, 3),
        "in_ctx_t": ctx.transpose(2, 0, 1),
        "in_probs": a["ctxb_2048x64"].reshape(B, 4, 128, P_PROG).transpose(2, 0, 1, 3),
        "in_mask": a["mask_BxS2_bf1"].reshape(1, B, S2).view(np.uint8),
        "in_w": w, "in_cols": cols, "in_rows": rows, "in_toks": toks,
        "in_ident": np.eye(128, dtype=f32),
        "in_dist": dist.astype(ml_dtypes.bfloat16),
        "in_slopes": slopes.astype(ml_dtypes.bfloat16),
        "in_tri": (i[:, None] >= i[None, :]).astype(f32),
        "in_qones": np.ones((1, 16 * T), ml_dtypes.bfloat16),
    }
    arrays = {k: np.ascontiguousarray(v) for k, v in arrays.items()}
    nc = bacc.Bacc("TRN2", target_bir_lowering=False, num_devices=1)
    args = [nc.dram_tensor(k, v.shape, mybir.dt.from_np(v.dtype), kind="ExternalInput").ap() for k, v in arrays.items()]
    out = nc.dram_tensor("out_dram", (B, T, D), F32, kind="ExternalOutput").ap()
    build_program(nc, *args, out)
    res = run_bass_kernel_spmd(nc, [arrays], core_ids=[0])
    return res.results[0]["out_dram"]
```

```python
from contextlib import ExitStack

import numpy as np

import concourse.bass as bass
from concourse import mybir

ALU = mybir.AluOpType
ACT = mybir.ActivationFunctionType
AX_X = mybir.AxisListType.X
F32 = mybir.dt.float32
BF16 = mybir.dt.bfloat16
U8 = mybir.dt.uint8

B, T, D = 2, 256, 128
S2 = 512
QT = T // 128
S_STATE, P_PROG, F_FF = 64, 64, 512
BIG = 1e30
PARTS = 3
TERM_ROWS = 96
MASK_ROW = 48
TERMS = 6
Q_TERM = [0, 0, 0, 1, 1, 2]
K_TERM = [0, 1, 2, 0, 1, 0]

HEADS = [16, 16, 8, 16, 16, 16]
KEYS = [T, S2, S2, T, S2, S2]
SA0, CA0, CA1, SA2, CA2, CA3 = range(6)
SCALE = [8 ** -0.5, 8 ** -0.5, 0.25, 1.0 / 16.0, 1.0, 8 ** -0.5]
UNITS = [(layer, b) for layer in range(6) for b in range(B)]

W_COLS = {}
_at = 0
for _n, _w in [("q0", 128), ("k0", 128), ("v0", 128), ("o0", 128), ("q1", 128), ("k1", 128), ("v1", 128), ("o1", 128),
               ("w12", 1024), ("w3", 512), ("q2", 128), ("k2", 128), ("v2", 128), ("o2", 128), ("win", 128),
               ("bmat", 64), ("at", 64), ("cmat", 128), ("prog", 128), ("q3", 128), ("k3", 128), ("v3", 128),
               ("q4", 128), ("k4", 128), ("v4", 128), ("f1", 128), ("f2", 128), ("q5", 128), ("k5", 128),
               ("v5", 128), ("o5", 128)]:
    W_COLS[_n] = (_at, _w)
    _at += _w
W_TOTAL = _at
W_FIRST = W_COLS["o0"][0]
W_NEXT = W_COLS["w12"][0]
ONES_AT = (0, 1, 2, 3, 4, 10)
COLS = ["bq0", "bk0", "bq1", "bk1", "bq2", "bk2", "bq3", "bk3", "bq4", "bk4", "g_ln1", "b_ln1", "g_ln2", "b_ln2",
        "g_x1", "b_x1", "g_x2", "b_x2", "b_in", "g_sa", "b_sa", "g_ca", "b_ca", "b_f1", "g_q", "g_c"] + \
       [f"b12_{i}" for i in range(8)]
COL = {n: i for i, n in enumerate(COLS)}
ROWS = ["bv0", "bo0", "bv1", "bo1", "b3", "bv2", "bo2", "bprog", "bv3", "bv4", "bf2"]
ROW = {n: i for i, n in enumerate(ROWS)}
TOKS = ["g_ln1", "b_ln1", "g_ln2", "b_ln2", "g_ln3", "b_ln3", "g_sa", "b_sa", "g_ca", "b_ca", "g_ffn", "b_ffn", "g_out"]
TOK = {n: i for i, n in enumerate(TOKS)}


def bf16_parts(x):
    parts = []
    x = np.float32(x)
    for _ in range(PARTS):
        p = np.float32((np.array(x, np.float32).view(np.uint32) & np.uint32(0xFFFF0000)).view(np.float32))
        if p != 0:
            parts.append(float(p))
        x = np.float32(x - p)
    return parts


SLOPES = (2.0 ** (-8.0 * np.arange(1, 17, dtype=np.float32) / 16)).astype(np.float32)
SLOPE_PARTS = [(h, p) for h in range(16) for p in bf16_parts(SLOPES[h])]
SLOPE_OF = [[n for n, (hh, _) in enumerate(SLOPE_PARTS) if hh == h] for h in range(16)]

GROUPS = [(u, g) for u, (layer, _) in enumerate(UNITS) for g in range(HEADS[layer] // 4)]
GROUP_AT = {ug: gi for gi, ug in enumerate(GROUPS)}
STEPS = [(gi, kt) for gi, (u, _) in enumerate(GROUPS) for kt in range(KEYS[UNITS[u][0]] // 128)]
STEP_AT = {s: n for n, s in enumerate(STEPS)}
RING = 3
WARM_UP = (8, 3, 2, 1)


def last_step(u):
    return max(n for n, (gi, _) in enumerate(STEPS) if GROUPS[gi][0] == u) + 1


def tiles(gi):
    n = S2 // KEYS[UNITS[GROUPS[gi][0]][0]]
    return [(qt, j, n) for qt in range(QT) for j in range(0, 4, n)]


def chain(u):
    layer = UNITS[u][0]
    norm = lambda tag: [("stats", u, tag), ("pow", u, tag), ("norm", u, tag)]
    nxt = u + 2
    query = [("qproj", nxt), ("qsplit", nxt), ("qload", nxt)]
    if layer == SA0:
        return [("attnT", u), ("oproj", u)] + norm("a") + [("nT", u, "a"), ("tok", u, "a")] + query
    if layer == CA0:
        return ([("attnT", u), ("oproj", u)] + norm("a") + [("nT", u, "a"), ("tok", u, "a")]
                + [("glu", u, f) for f in range(4)] + [("ffout", u)] + norm("b") + [("tokd", u, "b")]
                + norm("c") + [("nT", u, "c")] + query)
    if layer == CA1:
        return [("attnT", u), ("oproj", u)] + norm("a") + [("nT", u, "a"), ("win", u), ("uproj", u)]
    if layer == SA2:
        return [("zstore", u), ("zload", u), ("zadd", u)] + norm("a") + [("nT", u, "a"), ("tok", u, "a")] + query
    if layer == CA2:
        return ([("zstore", u), ("zload", u), ("zadd", u)] + norm("a") + [("nT", u, "a"), ("tok", u, "a"), ("relu", u), ("ffout", u)]
                + norm("b") + [("tokd", u, "b")] + norm("c") + [("nT", u, "c")] + query)
    return [("attnT", u), ("oproj", u)] + norm("a") + [("outmul", u), ("outstore", u)]


def layer_of(item):
    return UNITS[item[1]][0]


def parts(item):
    kind, layer = item[0], UNITS[GROUPS[item[1]][0]][0] if item[0] in ("scores", "shift", "finish") else None
    if kind == "scores":
        last = item[2] == len(tiles(item[1])) - 1
        return [("PE", 0.49 if layer == SA0 else 0.17), ("DVE", 0.82 + (0.35 if last else 0))]
    if kind == "step":
        return [("PE", 1.2 if UNITS[GROUPS[STEPS[item[1]][0]][0]][0] == SA0 else 0.39), ("ACT", 0.91)]
    if kind == "values":
        if UNITS[GROUPS[STEPS[item[1]][0]][0]][0] == SA2:
            return [("PE", 0.9)]
        return [("PE", 0.73)]
    wide = 2 if len(item) > 1 and kind in ("kproj", "ksplit", "vproj") and KEYS[UNITS[item[1]][0]] == S2 else 1
    return {
        "shift": [("PE", 0.2), ("ACT", 0.35), ("SP", 0.5), ("DMA", 2.0)],
        "triangle": [("POOL", 1.4)], "drain": [("ACT", 0.45)], "finish": [("PE", 0.3), ("DVE", 0.6)],
        "attnT": [("PE", 0.3), ("ACT", 0.5)], "oproj": [("PE", 0.7), ("DVE", 0.5)],
        "stats": [("DVE", 1.0)], "pow": [("POOL", 0.9)], "norm": [("DVE", 0.7)], "nT": [("PE", 0.3), ("ACT", 0.6)],
        "tok": [("POOL", 1.5)], "tokd": [("DVE", 0.9)],
        "qproj": [("PE", 0.5), ("DVE", 0.5)], "qsplit": [("DVE", 1.4)], 
        "qload": [("SP", 1.9), ("DMA", 2.0)],
        "kproj": [("PE", 0.5 * wide), ("ACT", 0.4 * wide if wide == 1 else 1.2)], "ksplit": [("DVE", 1.5) if kind == "ksplit" and layer_of(item) in (SA0, SA2) else ("POOL", 1.3)], "krest": [("POOL", 1.3), ("ACT", 0.7)],
        "kload": [("SP", 3.3), ("DMA", 2.2)],
        "vproj": [("PE", 0.6 * wide), ("ACT", 0.4 * wide)],
        "glu": [("PE", 0.9), ("ACT", 0.5), ("DVE", 1.3)], "ffout": [("PE", 2.0), ("DVE", 0.5)],
        "relu": [("PE", 0.5), ("ACT", 0.5)], "win": [("PE", 0.5), ("ACT", 0.5)], "uproj": [("PE", 0.5), ("ACT", 0.5)],
        "ssm": [("PE", 0.7), ("DVE", 0.5)], "xT": [("PE", 0.3), ("ACT", 0.5)],
        "ctxstats": [("DVE", 2.8), ("POOL", 3.5)], "cnorm": [("POOL", 4.0)], "cT": [("PE", 0.5), ("ACT", 0.7)],
        "mod1": [("PE", 0.5), ("ACT", 0.3)], "mod2": [("PE", 0.5), ("ACT", 0.3)], "maskprep": [("DVE", 1.8)], "flag": [("PE", 0.2), ("ACT", 0.3)],
        "zstore": [("SP", 1.0), ("DMA", 4.0)], "zload": [("SP", 0.5), ("DMA", 2.5)], "zadd": [("DVE", 0.5)],
        "outmul": [("DVE", 0.5)], "outstore": [("SP", 0.1)],
        "scan": [("PE", 165.0)],
        "inputs": [("SP", 2.4)], "warm": [("PE", 0.2)], "idb": [("DVE", 0.2)], "clear": [("POOL", 3.8)], "vclear": [("POOL", 1.2)], "kclear": [("POOL", 7.0)],
    }[kind]


def needs():
    n = {}

    def line(items, *first):
        before = list(first)
        for item in items:
            n.setdefault(item, []).extend(before)
            before = [item]

    last_group = lambda u: GROUP_AT[(u, HEADS[UNITS[u][0]] // 4 - 1)]
    last_values = lambda u: ("values", last_step(u) - 1)
    for gi, (u, g) in enumerate(GROUPS):
        layer, b = UNITS[u]
        for i in range(len(tiles(gi))):
            line([("scores", gi, i)], ("qload", u), ("kload", u), *([("scores", gi, i - 1)] if i else [("scores", gi - 1, len(tiles(gi - 1)) - 1)] if gi else []))
        line([("shift", gi)], ("scores", gi, len(tiles(gi)) - 1), *([("shift", gi - 1)] if gi else []))
        for kt in range(KEYS[layer] // 128):
            s = STEP_AT[(gi, kt)]
            line([("step", s)], ("shift", gi), *([("step", s - 1)] if s else []))
            if layer == SA2:
                line([("triangle", s), ("values", s)], ("step", s), *([("triangle", s - 1)] if kt or g or b else []))
            line([("values", s)], ("step", s), ("vproj", u), *([("values", s - 1)] if s else []))
        line([("drain", gi), ("finish", gi)], last_values_of(gi), *([("drain", gi - 1)] if gi else []), *([("finish", gi - 1)] if gi else []))
    for s in range(len(STEPS)):
        gi, kt = STEPS[s]
        if s >= 2:
            line([("step", s)], ("step", s - 2))
        if s >= 3:
            line([("step", s)], ("values", s - 3))
        if kt == 0 and gi:
            line([("values", s)], ("drain", gi - 1))
    for u, (layer, b) in enumerate(UNITS):
        c = [x for x in chain(u) if x[0] != "tok"]
        glus = [x for x in c if x[0] == "glu"]
        if glus:
            at = c.index(glus[0])
            line(c[:at], ("finish", last_group(u)))
            line(c[at + 4:], *glus)
            for f, x in enumerate(glus):
                line([x], c[at - 1], *([glus[f - 2]] if f >= 2 else []))
        else:
            line(c, ("finish", last_group(u)))
        for x in chain(u):
            if x[0] == "tok":
                line([x], ("norm", u, "a"))
                line([("ffout", u)] if layer in (CA0, CA2) else [("zadd" if layer == SA2 else "oproj", u + 2)], x)
    for u in (0, 1):
        line([("qproj", u), ("qsplit", u), ("qload", u)])
    line([("clear", "q0"), ("clear", "k0"), ("vclear", 0), ("clear", "q1"), ("clear", "k1"), ("vclear", 1), ("kclear", 0), ("vclear", 2),
          ("kclear", 1), ("vclear", 3), ("vclear", 4), ("vclear", 5), ("clear", "late")])
    for item, what in ((("qload", 0), "q0"), (("kload", 0), "k0"), (("qload", 1), "q1"), (("kload", 1), "k1"), (("kload", 4), "late")):
        line([item], ("clear", what))
    line([("inputs", 0), ("inputs", 1)], ("kload", 0))
    line([("idb",)], ("ksplit", 0))
    line([("shift", 0)], ("idb",))
    line([("oproj", 0)], ("inputs", 0))
    line([("kproj", 2)], ("inputs", 0))
    line([("ctxstats",)], ("inputs", 1))
    line([("glu", 2, 0)], ("inputs", 1))
    for u in range(6):
        line([("vproj", u)], ("vclear", u))
    for b in range(B):
        line([("kload", 2 + b)], ("kclear", b))
    order = [0, 1, 2, 3, 4, 5, 8, 9, 6, 7, 10, 11]
    source = {6: [("xT", 0)], 7: [("xT", 1)], 4: [("cT", 4)], 5: [("cT", 5)], 10: [("cT", 10)], 11: [("cT", 11)]}
    for i, u in enumerate(order):
        line([("kproj", u), *([] if UNITS[u][0] in (SA0, SA2) else [("krest", u)]), ("ksplit", u), ("kload", u)], *source.get(u, []), *([("ksplit", order[i - 1])] if i else []))
        line([("vproj", u)], *source.get(u, []))
    line([("kload", 5)], last_values(0))
    for b in range(B):
        line([("kload", 2 * CA2 + b)], last_values(2 * CA0 + b))
        line([("vproj", 2 * SA2 + b)], ("mod1",))
        line([("vproj", 2 * CA2 + b)], last_values(2 * CA0 + b))
        line([("vproj", 2 * CA3 + b)], ("flag",))
    line([("kload", 10)], ("maskprep",))
    line([("kload", 11)], ("maskprep",), last_values(7))
    contexts = [4, 5, 10, 11]
    line([("ctxstats",)], ("kproj", 1))
    for i, u in enumerate(contexts):
        line([("cnorm", u), ("cT", u)], ("ctxstats",))
        if i:
            line([("cnorm", u)], ("cT", contexts[i - 1]))
            line([("cT", u)], ("kproj", contexts[i - 1]), ("vproj", contexts[i - 1]))
    line([("mod1",), ("mod2",)], last_values(1))
    line([("maskprep",), ("flag",)], ("oproj", 1))
    for f in range(4):
        line([("glu", 3, f)], ("ffout", 2))
    line([("relu", 9)], ("ffout", 8))
    line([("win", 4)], ("ffout", 3))
    line([("win", 5)], ("uproj", 4))
    line([("oproj", 5), ("warm", 0), ("nT", 5, "a"), ("warm", 1), ("win", 5), ("warm", 2), ("uproj", 5), ("warm", 3), ("scan",)])
    line([("scan",)], ("uproj", 4), ("uproj", 5), ("finish", last_group(5)), ("mod2",), ("vproj", 9), ("kload", 9))
    for b in range(B):
        line([("ssm", b), ("xT", b), ("qproj", 2 * SA2 + b), ("qsplit", 2 * SA2 + b), ("qload", 2 * SA2 + b)], ("scan",))
    line([("cnorm", 10)], ("scan",))
    return n


def last_values_of(gi):
    return ("values", STEP_AT[(gi, KEYS[UNITS[GROUPS[gi][0]][0]] // 128 - 1)])


IN_RING = {"scores", "shift", "finish", "attnT", "oproj", "nT", "qproj", "kproj", "vproj", "glu", "ffout", "relu",
           "win", "uproj", "ssm", "xT", "cT", "mod1", "mod2", "flag"}
FIRST = {"step": 0.03, "values": -0.6, "shift": 1.24, "finish": 0.5, "drain": 0.5, "triangle": -0.6, "scores": 0.0}
CHAIN_FIRST, EXTRA_FIRST = 0.51, -0.45
AHEAD = 3
IDLE = 0.3
LEAD = 4
HOP = 0.25


def schedule():
    need = needs()
    done, free, ring, uses, out = {}, {}, [0.0] * RING, 0, []
    extra = {k for k in need if k[0] in ("kproj", "krest", "ksplit", "kload", "vproj", "cnorm", "cT", "ctxstats", "mod1", "mod2", "maskprep", "flag")
             and (len(k) == 1 or UNITS[k[1]][0] not in (SA0, SA2))}
    left = dict(need)
    at_group = 0
    exp_end, val_end, fin_act = {}, {}, {}
    while left:
        best = None
        for item, before in left.items():
            if any(x not in done for x in before):
                continue
            kind = item[0]
            if kind == "scores" and item[1] > at_group + AHEAD:
                continue
            if item in extra and kind in ("kproj", "cnorm") and GROUPS[min(at_group, len(GROUPS) - 1)][0] < (item[1] - LEAD if item[1] < 8 else item[1] - 4):
                continue
            t = 0.0
            for x in before:
                if not (kind == "step" and x[0] in ("step", "values")) and not (kind in ("values", "scores") and x[0] == "drain") \
                        and not (kind == "values" and x[0] == "values") and not (kind == "scores" and x[0] == "scores") and not (kind == "shift" and x[0] == "shift"):
                    t = max(t, done[x] - (1.3 if kind == "ffout" and x[0] == "glu" else 0.0))
            marks, idle, first, ready = [], 0.0, None, t
            for k, (engine, length) in enumerate(parts(item)):
                if engine == "DMA":
                    t += length
                    continue
                if kind == "step" and k == 0 and item[1] >= 2:
                    t = max(t, exp_end[item[1] - 2])
                if kind == "step" and k == 1 and item[1] >= 3:
                    t = max(t, val_end[item[1] - 3])
                if kind == "values" and STEPS[item[1]][1] == 0 and STEPS[item[1]][0]:
                    t = max(t, fin_act[STEPS[item[1]][0] - 1])
                if engine == "PE" and kind in IN_RING:
                    t = max(t, ring[uses % RING])
                s = max(t + (HOP if k else 0), free.get(engine, 0.0))
                if k:
                    if engine != "SP":
                        idle += s - max(free.get(engine, 0.0), first)
                else:
                    first = s
                    if engine == "PE":
                        ready = s
                marks.append((engine, s + length))
                t = s + length
            cost = ready + IDLE * min(idle, 3.0) - (FIRST[kind] if kind in FIRST else EXTRA_FIRST if item in extra else CHAIN_FIRST)
            if best is None or cost < best[0]:
                best = (cost, item, marks, t)
        assert best, list(left)[:20]
        _, item, marks, t = best
        kind = item[0]
        for engine, end in marks:
            free[engine] = end
        if kind in IN_RING:
            ring[uses % RING] = marks[-1][1] if kind != "shift" else marks[1][1]
            uses += 1
        if kind == "scan":
            for e in ("PE", "ACT", "DVE", "POOL"):
                free[e] = marks[0][1]
        if kind == "step":
            exp_end[item[1]] = marks[1][1]
        if kind == "values":
            val_end[item[1]] = marks[-1][1]
        if kind == "finish":
            at_group = item[1] + 1
        if kind == "drain":
            fin_act[item[1]] = marks[0][1]
        done[item] = t + HOP
        del left[item]
        out.append(item)
    return out




SCHED = schedule()
BANK = {}
_uses = [0] * RING
for _i in SCHED:
    if _i[0] in IN_RING:
        assert _i not in BANK, _i
        _k = len(BANK) % RING
        BANK[_i] = (_k, _uses[_k])
        _uses[_k] += 1
IN_CHAIN = {"stats", "pow", "norm", "tokd", "zadd", "outmul"}
CHAIN = {}
_n = [0] * B
for _i in SCHED:
    if _i[0] in IN_CHAIN:
        _b = UNITS[_i[1]][1]
        _n[_b] += 1
        CHAIN[_i] = _n[_b]
SIDE = {}
_n = [0] * B
for _i in SCHED:
    if _i[0] == "tok":
        _b = UNITS[_i[1]][1]
        _n[_b] += 1
        SIDE[_i] = _n[_b]
CLEARED = {}
for _i in SCHED:
    if _i[0] == "clear":
        CLEARED[_i] = max(CLEARED.values(), default=0) + (1 if _i[1] == "late" else 2)
KSPLITS = [i[1] for i in SCHED if i[0] == "ksplit"]
KRESTS = [i[1] for i in SCHED if i[0] == "krest"]
CNORMS = [i[1] for i in SCHED if i[0] == "cnorm"]

NORM_COLS = {(SA0, "a"): ("g_ln1", "b_ln1"), (CA0, "a"): ("g_ln2", "b_ln2"), (CA0, "c"): ("g_x1", "b_x1"),
             (CA1, "a"): ("g_x2", "b_x2"), (SA2, "a"): ("g_sa", "b_sa"), (CA2, "a"): ("g_ca", "b_ca"),
             (CA2, "c"): ("g_q", None)}
NORM_TOKS = {(SA0, "a"): ("g_ln1", "b_ln1"), (CA0, "a"): ("g_ln2", "b_ln2"), (CA0, "b"): ("g_ln3", "b_ln3"),
             (SA2, "a"): ("g_sa", "b_sa"), (CA2, "a"): ("g_ca", "b_ca"), (CA2, "b"): ("g_ffn", "b_ffn")}
RMS = {(CA2, "c"), (CA3, "a")}
FROM_X = {(CA0, "c"), (CA1, "a"), (CA2, "c")}
EPS = {True: 1e-6, False: 1e-5}


def build_program(nc, x_tok, x_t, ctx_tok, ctx_t, probs, mask, w, cols, rows, toks, ident, dist, slopes, tri, ones, out):
    with ExitStack() as stack:
        def sb(name, shape, dt=F32):
            return stack.enter_context(nc.sbuf_tensor(name, shape, dt))

        def sem(name):
            return stack.enter_context(nc.semaphore(name))

        w_sb = sb("w_sb", [128, W_TOTAL])
        col_sb = sb("col_sb", [128, len(COLS)])
        row_sb = sb("row_sb", [1, len(ROWS), 128])
        tok_sb = sb("tok_sb", [128, len(TOKS), 128])
        id_sb = sb("id_sb", [128, 128])
        idb_sb = sb("idb_sb", [128, 128], BF16)
        dist_sb = sb("dist_sb", [128, 2, T], BF16)
        tri_sb = sb("tri_sb", [128, 128])
        ones_row = sb("ones_row", [1, 128])
        inv_col = sb("inv_col", [128, 1])
        xT_in = sb("xT_in", [128, B, T])
        ctxT_sb = sb("ctxT_sb", [128, B, S2])
        ctx_sb = sb("ctx_sb", [128, B, 4, 128])
        probs_sb = sb("probs_sb", [128, B, 4, P_PROG])
        mask_sb = sb("mask_sb", [1, B, S2], U8)
        flag_row = sb("flag_row", [1, B])
        flag = sb("flag", [128, B])
        pmean = sb("pmean", [P_PROG, B])
        modrow = sb("modrow", [1, B, 128])
        q_pack = [sb(f"q_pack{b}", [128, 16 * T], BF16) for b in range(B)]
        k_even = [sb(f"k_even{b}", [128, 16 * S2], BF16) for b in range(B)]
        k_odd = [sb(f"k_odd{b}", [128, 16 * S2], BF16) for b in range(B)]
        slope_sb = k_odd[0][:, 8 * S2:8 * S2 + len(SLOPE_PARTS) * 128].rearrange("p (n c) -> p n c", c=128)
        v_self = [sb(f"v_self{b}", [128, 2 * 16 * 16]) for b in range(B)]
        v_even = [sb(f"v_even{b}", [128, 4 * 16 * 16]) for b in range(B)]
        v_odd = [sb(f"v_odd{b}", [128, 4 * 16 * 16]) for b in range(B)]
        den_sb = sb("den_sb", [128, 16])
        probs_e = [sb(f"probs_e{i}", [128, 4 * T]) for i in range(3)]
        probs_m = [sb(f"probs_m{i}", [128, 4, 128]) for i in range(2)]
        rowmax = [sb(f"rowmax{i}", [128, QT, 4]) for i in range(2)]
        shift_p = [sb(f"shift_p{i}", [128, QT, 2, 4], BF16) for i in range(2)]
        shift_t = [sb(f"shift_t{i}", [8, T], BF16) for i in range(4)]
        o_sb = [sb(f"o_sb{i}", [128, T]) for i in range(2)]
        rden = sb("rden", [128, QT, 4, 1])
        X = [sb(f"X{b}", [128, QT, D]) for b in range(B)]
        r = [sb(f"r{b}", [128, QT, D]) for b in range(B)]
        nrm = [sb(f"nrm{b}", [128, QT, D]) for b in range(B)]
        attn = [sb(f"attn{b}", [128, QT, D]) for b in range(B)]
        XT = [sb(f"XT{b}", [128, T]) for b in range(B)]
        z = [sb(f"z{b}", [128, QT, D]) for b in range(B)]
        attnT = [z[b][:, :, :].rearrange("p t d -> p (t d)") for b in range(B)]
        qf = [sb(f"qf{b}", [128, T]) for b in range(B)]
        qr = [sb(f"qr{b}", [128, T]) for b in range(B)]
        glu_t = [(attnT[b], r[b][:, :, :].rearrange("p t d -> p (t d)")) for b in range(B)]
        glu_a, glu_w = qf, qr
        qp = [sb(f"qp{b}", [128, PARTS, T], BF16) for b in range(B)]
        kf = sb("kf", [128, S2])
        kp = [sb(f"kp{i}", [128, PARTS, S2], BF16) for i in range(2)]
        stats = [sb(f"stats{b}", [128, QT, 6]) for b in range(B)]
        mv = [sb(f"mv{b}", [128, QT, 2]) for b in range(B)]
        ve = [sb(f"ve{b}", [128, QT]) for b in range(B)]
        rs = [sb(f"rs{b}", [128, QT]) for b in range(B)]
        half = sb("half", [128, 8])
        half_b = sb("half_b", [128, 4])
        cstats = sb("cstats", [128, 8, 6])
        cmv = sb("cmv", [128, 8, 2])
        cve = sb("cve", [128, 2, 8])
        crs = sb("crs", [128, 2, 8])
        cn = sb("cn", [128, 4, 128])
        cT = sb("cT", [128, S2])
        hT = sb("hT", [128, 4, T])
        mrow = w_sb[0:1, 0:B * S2 // 2].bitcast(BF16).rearrange("p (b t) -> p b t", b=B)
        UT = w_sb[0:S_STATE, 1024:1024 + T * B].rearrange("p (t b) -> p t b", b=B)
        G = w_sb[0:S_STATE, 1536:1536 + T * B].rearrange("p (t b) -> p t b", b=B)

        ring = [stack.enter_context(nc.psum_tensor(f"ring{k}", [128, 512], F32)) for k in range(RING)]
        st_ps = [stack.enter_context(nc.psum_tensor(f"st_ps{i}", [128, 1024], F32)) for i in range(2)]
        o_ps = stack.enter_context(nc.psum_tensor("o_ps", [128, 512], F32))
        scan_ps = st_ps[0][0:S_STATE, 0:512]

        z_dram = {u: nc.dram_tensor(f"z_scratch{u}", (16, T, 8), F32).ap() for u in range(12) if UNITS[u][0] in (SA2, CA2)}

        in_first = sem("in_first")
        in_ident = sem("in_ident")
        in_const = sem("in_const")
        in_ctx = sem("in_ctx")
        in_next = sem("in_next")
        in_rest = sem("in_rest")
        consts_set = sem("consts_set")
        idb_done = sem("idb_done")
        half_set = sem("half_set")
        cleared = sem("cleared")
        keys_cleared = sem("keys_cleared")
        values_cleared = sem("values_cleared")
        late_cleared = sem("late_cleared")
        ones_cleared = sem("ones_cleared")
        bank_full = [sem(f"bank_full{k}") for k in range(RING)]
        bank_free = [sem(f"bank_free{k}") for k in range(RING)]
        chain_s = [sem(f"chain{b}") for b in range(B)]
        q_parts = [sem(f"q_parts{b}") for b in range(B)]
        side_s = [sem(f"side{b}") for b in range(B)]
        dve_step = sem("dve_step")
        pool_step = sem("pool_step")
        q_landed = [sem(f"q_landed{u}") for u in range(12)]
        k_landed = [sem(f"k_landed{u}") for u in range(12)]
        z_stored = {u: sem(f"z_stored{u}") for u in z_dram}
        z_landed = {u: sem(f"z_landed{u}") for u in z_dram}
        keys_rest = sem("keys_rest")
        keys_second = sem("keys_second")
        keys_split = sem("keys_split")
        shift_ready = sem("shift_ready")
        shift_landed = [sem(f"shift_landed{i}") for i in range(4)]
        st_full = sem("st_full")
        exp_done = sem("exp_done")
        masked = sem("masked")
        values_done = sem("values_done")
        o_taken = sem("o_taken")
        gate_done = sem("gate_done")
        cstats_done = sem("cstats_done")
        crs_done = sem("crs_done")
        cn_done = sem("cn_done")
        mask_done = sem("mask_done")
        scan_pre = sem("scan_pre")
        scan_h = sem("scan_h")
        scan_g = sem("scan_g")
        states_done = sem("states_done")
        out_landed = sem("out_landed")

        def W(name, k=128):
            at, n = W_COLS[name]
            return w_sb[0:k, at:at + n]

        def C(name):
            return col_sb[:, COL[name]:COL[name] + 1]

        def v_pack(u):
            layer, b = UNITS[u]
            t = (v_self if layer in (SA0, SA2) else v_even if layer in (CA0, CA2) else v_odd)[b]
            return t[:, :].rearrange("p (t h c) -> p t h c", h=HEADS[layer], c=16 if HEADS[layer] == 16 else 32)

        def k_rows(u, first, end):
            layer, b = UNITS[u]
            if layer in (SA0, SA2):
                return k_odd[1][first:end, b * 16 * T:(b + 1) * 16 * T]
            return (k_odd if layer in (CA1, CA3) else k_even)[b][first:end, :]

        def q_rows(u, first, end):
            return q_pack[UNITS[u][1]][first:end, :]

        def head_dim(u):
            return D // HEADS[UNITS[u][0]]

        def claim(e, key):
            k, n = BANK[key]
            if n:
                e.wait_ge(bank_free[k], n)
            return ring[k]

        def filled(e, key):
            k, n = BANK[key]
            e.wait_ge(bank_full[k], n + 1)
            return ring[k]

        def taken(e, key):
            k, n = BANK[key]
            e.wait_ge(bank_free[k], n + 1)

        def full(key):
            return bank_full[BANK[key][0]]

        def free(key):
            return bank_free[BANK[key][0]]

        def landings(u):
            return 16 * (TERMS + (u in ONES_AT) + (UNITS[u][0] == CA3))

        def keys_free(e, i):
            if i >= 2:
                e.wait_ge(k_landed[KSPLITS[i - 2]], landings(KSPLITS[i - 2]))

        def loaded(e, layer):
            if layer == SA0:
                e.wait_ge(in_first, 64)
            elif layer == CA0:
                e.wait_ge(in_next, 64)
            else:
                e.wait_ge(in_rest, 80)

        def chained(e, key):
            e.wait_ge(chain_s[UNITS[key[1]][1]], CHAIN[key])

        def source_ready(e, u):
            layer, b = UNITS[u]
            if layer == SA0:
                e.wait_ge(in_first, 64)
            elif layer == SA2:
                taken(e, ("xT", b))
            else:
                taken(e, ("nT", u - 2, {CA0: "a", CA1: "c", CA2: "a", CA3: "c"}[layer]))

        def query_source(u):
            layer, b = UNITS[u]
            return xT_in[:, b, :] if layer == SA0 else XT[b][:, :]

        def key_source(e, u):
            layer, b = UNITS[u]
            if layer in (SA0, SA2):
                source_ready(e, u)
                return query_source(u)
            if layer in (CA0, CA2):
                e.wait_ge(in_ctx, 16)
                return ctxT_sb[:, b, :]
            taken(e, ("cT", u))
            return cT[:, :]

        block = stack.enter_context(nc.Block())

        @block.sync
        def _(sp):
            sp.dma_start(w_sb[:, 0:W_FIRST], w[:, 0:W_FIRST]).then_inc(in_first, 16)
            sp.dma_start(xT_in[:, :, :], x_t).then_inc(in_first, 16)
            sp.dma_start(col_sb[:, :], cols).then_inc(in_first, 16)
            sp.dma_start(row_sb[:, :, :], rows).then_inc(in_first, 16)
            sp.dma_start(id_sb[:, :], ident).then_inc(in_ident, 16)
            sp.dma_start(dist_sb[:, :, :], dist).then_inc(in_const, 16)
            sp.dma_start(slope_sb, slopes).then_inc(in_const, 16)

            for item in SCHED:
                kind = item[0]
                if kind == "inputs":
                    if item[1] == 0:
                        sp.dma_start(ctxT_sb[:, :, :], ctx_t).then_inc(in_ctx, 16)
                        sp.dma_start(w_sb[:, W_FIRST:W_NEXT], w[:, W_FIRST:W_NEXT]).then_inc(in_next, 16)
                        for b in range(B):
                            sp.dma_start(X[b][:, :, :], x_tok[b]).then_inc(in_next, 16)
                        sp.dma_start(tok_sb[:, :, :], toks).then_inc(in_next, 16)
                    else:
                        sp.dma_start(w_sb[:, W_NEXT:W_TOTAL], w[:, W_NEXT:W_TOTAL]).then_inc(in_rest, 16)
                        sp.dma_start(ctx_sb[:, :, :, :], ctx_tok).then_inc(in_rest, 16)
                        sp.dma_start(probs_sb[:, :, :, :], probs).then_inc(in_rest, 16)
                        sp.dma_start(mask_sb[:, :, :], mask).then_inc(in_rest, 16)
                        sp.dma_start(tri_sb[:, :], tri).then_inc(in_rest, 16)
                elif kind == "qload":
                    u = item[1]
                    layer, b = UNITS[u]
                    hd = head_dim(u)
                    if layer == SA0:
                        sp.wait_ge(cleared, CLEARED[("clear", f"q{b}")])
                    if layer == SA2:
                        sp.wait_ge(late_cleared, 2)
                    for n in range(TERMS):
                        if n == 0 or Q_TERM[n] != Q_TERM[n - 1]:
                            sp.wait_ge(q_parts[b], PARTS * layer + Q_TERM[n] + 1)
                        sp.dma_start(q_rows(u, n * hd, (n + 1) * hd)[:, 0:HEADS[layer] * T].rearrange("p (h t) -> p h t", t=T),
                                     qp[b][:, Q_TERM[n], :]).then_inc(q_landed[u], 16)
                    if layer == SA2:
                        sp.dma_start(q_rows(u, MASK_ROW, MASK_ROW + 1), ones[0:1, 0:16 * T]).then_inc(q_landed[u], 16)
                elif kind == "kload":
                    u = item[1]
                    layer, b = UNITS[u]
                    hd, n_keys = head_dim(u), KEYS[layer]
                    sp.wait_ge(keys_split, KSPLITS.index(u) + 1)
                    if layer == SA0:
                        sp.wait_ge(cleared, CLEARED[("clear", f"k{b}")])
                    if u == 4:
                        sp.wait_ge(cleared, CLEARED[("clear", "late")])
                    if layer == CA1 and b == 1:
                        sp.wait_ge(st_full, last_step(2 * SA0))
                    if layer == CA0:
                        sp.wait_ge(keys_cleared, 2 * (b + 1))
                    if layer == SA2:
                        sp.wait_ge(late_cleared, 2)
                    if layer == CA2:
                        sp.wait_ge(st_full, last_step(2 * CA0 + b))
                    if layer == CA3:
                        sp.wait_ge(late_cleared, 4)
                        sp.wait_ge(mask_done, 2)
                        if b == 1:
                            sp.wait_ge(st_full, last_step(2 * SA2 + 1))
                    for n in range(TERMS):
                        sp.dma_start(k_rows(u, n * hd, (n + 1) * hd)[:, 0:HEADS[layer] * n_keys].rearrange("p (h t) -> p h t", t=n_keys),
                                     kp[KSPLITS.index(u) % 2][:, K_TERM[n], 0:n_keys]).then_inc(k_landed[u], 16)
                    if u in ONES_AT:
                        sp.dma_start(k_rows(u, TERM_ROWS, TERM_ROWS + 2)[:, 0:HEADS[layer] * n_keys], ones[:, 0:HEADS[layer] * n_keys]).then_inc(k_landed[u], 16)
                    if layer == CA3:
                        sp.dma_start(k_rows(u, MASK_ROW, MASK_ROW + 1).rearrange("p (h t) -> p h t", t=n_keys),
                                     mrow[:, b, :].unsqueeze(1).broadcast_to([1, 16, n_keys])).then_inc(k_landed[u], 16)
                elif kind == "shift":
                    gi = item[1]
                    u, g = GROUPS[gi]
                    at = TERM_ROWS
                    taken(sp, item)
                    sp.dma_start(q_rows(u, at, at + 2)[:, 4 * g * T:4 * (g + 1) * T], shift_t[gi % 4][:, :]).then_inc(shift_landed[gi % 4], 16)
                elif kind == "zstore":
                    u = item[1]
                    b = UNITS[u][1]
                    taken(sp, ("finish", GROUP_AT[(u, 3)]))
                    for qt in range(QT):
                        sp.dma_start(z_dram[u][:, qt * 128:(qt + 1) * 128, :].rearrange("h s d -> s h d"),
                                     attn[b][:, qt, :].rearrange("p (h d) -> p h d", d=8)).then_inc(z_stored[u], 16)
                elif kind == "zload":
                    u = item[1]
                    b = UNITS[u][1]
                    sp.wait_ge(z_stored[u], 32)
                    sp.dma_start(z[b][:, :, :], z_dram[u].rearrange("(t h) (a r) d -> (h a) t (r d)", t=QT, r=16)).then_inc(z_landed[u], 16)
                elif kind == "outstore":
                    u = item[1]
                    b = UNITS[u][1]
                    chained(sp, ("outmul", u))
                    sp.dma_start(out[b].rearrange("(t p) d -> p t d", p=128), nrm[b][:, :, :]).then_inc(out_landed, 16)
            sp.wait_ge(out_landed, 16 * B)

        @block.tensor
        def _(pe):
            pe.wait_ge(consts_set, 2)

            def bias_rows(dst, name, n):
                for i in range(n):
                    pe.matmul(dst[:, i * 128:(i + 1) * 128], ones_row[:, :], row_sb[:, ROW[name], :], start=(i == 0), stop=False, skip_group_check=True)

            def turn(key, src):
                dst = claim(pe, key)
                for qt in range(QT):
                    last = nc.tensor.transpose(dst[:, qt * 128:(qt + 1) * 128], src[:, qt, :], id_sb[:, :])
                last.then_inc(full(key), 1)

            def scores(gi, i):
                u, g = GROUPS[gi]
                layer, b = UNITS[u]
                qt, j0, n = tiles(gi)[i]
                rows_n, n_keys = TERM_ROWS, KEYS[layer]
                if g == 0 and i == 0:
                    pe.wait_ge(q_landed[u], 16 * (TERMS + (layer == SA2)))
                    pe.wait_ge(k_landed[u], landings(u))
                    if layer == SA0:
                        pe.wait_ge(in_const, 32)
                dst = claim(pe, ("scores", gi, i))
                for j in range(n):
                    h = 4 * g + j0 + j
                    to = dst[:, j * n_keys:(j + 1) * n_keys]
                    last = nc.tensor.matmul(to, q_rows(u, 0, rows_n)[:, h * T + qt * 128:h * T + (qt + 1) * 128],
                                            k_rows(u, 0, rows_n)[:, h * n_keys:(h + 1) * n_keys], start=True, stop=(layer != SA0))
                    if layer == SA0:
                        for p in SLOPE_OF[h]:
                            last = nc.tensor.matmul(to, slope_sb[:, p, :], dist_sb[:, qt, :], start=False, stop=(p == SLOPE_OF[h][-1]))
                last.then_inc(full(("scores", gi, i)), 1)

            def shift(gi):
                dst = claim(pe, ("shift", gi))
                pe.wait_ge(shift_ready, gi + 1)
                for qt in range(QT):
                    last = nc.tensor.transpose(dst[0:8, qt * 64:(qt + 1) * 64].bitcast(BF16),
                                               shift_p[gi % 2][:, qt, :, :].rearrange("p a h -> p (a h)"), idb_sb[:, :])
                last.then_inc(full(("shift", gi)), 1)

            def step(n):
                gi, kt = STEPS[n]
                u, g = GROUPS[gi]
                layer, b = UNITS[u]
                rows_n, n_keys = 128, KEYS[layer]
                if kt == 0:
                    pe.wait_ge(shift_landed[gi % 4], 16 * (gi // 4 + 1))
                if n >= 2:
                    pe.wait_ge(exp_done, n - 1)
                dst = st_ps[n % 2]
                for j in range(4):
                    h = 4 * g + j
                    to = dst[:, j * T:(j + 1) * T]
                    last = nc.tensor.matmul(to, k_rows(u, 0, rows_n)[:, h * n_keys + kt * 128:h * n_keys + (kt + 1) * 128],
                                            q_rows(u, 0, rows_n)[:, h * T:(h + 1) * T], start=True, stop=(layer != SA0))
                    if layer == SA0:
                        for p in SLOPE_OF[h]:
                            last = nc.tensor.matmul(to, slope_sb[:, p, :], dist_sb[:, kt, :], start=False, stop=(p == SLOPE_OF[h][-1]))
                last.then_inc(st_full, 1)

            def values(n):
                gi, kt = STEPS[n]
                u, g = GROUPS[gi]
                layer, b = UNITS[u]
                v = v_pack(u)
                wide = v.shape[3]
                last_kt = KEYS[layer] // 128 - 1
                pe.wait_ge(exp_done, n + 1)
                if kt == 0:
                    if g == 0:
                        taken(pe, ("vproj", u))
                        if layer == SA2:
                            pe.wait_ge(ones_cleared, b + 1)
                    if gi:
                        pe.wait_ge(o_taken, gi)
                e = probs_e[n % 3]
                if layer == SA2:
                    for j in range(4):
                        to = o_ps[32 * j:32 * j + wide, 0:T]
                        nc.tensor.matmul(to, den_sb[:, :], e[:, j * T:(j + 1) * T], start=(kt == 0), stop=False, skip_group_check=True)
                    if kt == 1:
                        for j in range(4):
                            nc.tensor.matmul(o_ps[32 * j:32 * j + wide, 0:128], v[:, kt, 4 * g + j, :], e[:, j * T:j * T + 128],
                                             start=False, stop=False, skip_group_check=True)
                    pe.wait_ge(masked, MASKED_AT[n] + 1)
                    for j in range(4):
                        last = nc.tensor.matmul(o_ps[32 * j:32 * j + wide, kt * 128:(kt + 1) * 128], v[:, kt, 4 * g + j, :],
                                                probs_m[n % 2][:, j, :], start=False, stop=(kt == last_kt), skip_group_check=True)
                else:
                    for j in range(4):
                        last = nc.tensor.matmul(o_ps[32 * j:32 * j + wide, 0:T], v[:, kt, 4 * g + j, :], e[:, j * T:(j + 1) * T],
                                                start=(kt == 0), stop=(kt == last_kt), skip_group_check=True)
                last.then_inc(values_done, 1)

            def keep_clock(n):
                for _ in range(n):
                    nc.tensor.matmul(st_ps[1][:, 0:512], idb_sb[:, :], dist_sb[:, :, :].rearrange("p t k -> p (t k)"), start=True, stop=True)

            def scan():
                for b in range(B):
                    taken(pe, ("uproj", 2 * CA1 + b))
                pe.wait_ge(exp_done, last_step(2 * CA1 + 1))
                nc.tensor.matmul(scan_ps, W("at", S_STATE), UT[:, :, :].rearrange("p t b -> p (t b)"),
                                 start=True, stop=False, skip_group_check=True).then_inc(scan_pre, 1)
                for t in range(2, T):
                    pe.wait_ge(scan_g, t - 1)
                    nc.tensor.matmul(scan_ps[:, (t - 1) * B:t * B], W("at", S_STATE), G[:, t - 1, :], start=False,
                                     stop=(t == T - 1), skip_group_check=True).then_inc(scan_h, 1)
                    keep_clock(1)

            for item in SCHED:
                kind = item[0]
                if kind == "scores":
                    scores(item[1], item[2])
                elif kind == "shift":
                    shift(item[1])
                elif kind == "step":
                    step(item[1])
                elif kind == "values":
                    values(item[1])
                elif kind == "finish":
                    gi = item[1]
                    dst = claim(pe, item)
                    pe.wait_ge(o_taken, gi + 1)
                    for qt in range(QT):
                        last = nc.tensor.transpose(dst[:, qt * 128:(qt + 1) * 128], o_sb[gi % 2][:, qt * 128:(qt + 1) * 128], id_sb[:, :])
                    last.then_inc(full(item), 1)
                elif kind == "attnT":
                    u = item[1]
                    taken(pe, ("finish", GROUP_AT[(u, HEADS[UNITS[u][0]] // 4 - 1)]))
                    turn(item, attn[UNITS[u][1]])
                elif kind == "oproj":
                    u = item[1]
                    layer, b = UNITS[u]
                    loaded(pe, max(layer, CA0))
                    dst = claim(pe, item)
                    if layer != CA3:
                        bias_rows(dst, f"bo{layer}", QT)
                    taken(pe, ("attnT", u))
                    for qt in range(QT):
                        to = dst[:, qt * 128:(qt + 1) * 128]
                        last = nc.tensor.matmul(to, attnT[b][:, qt * 128:(qt + 1) * 128], W(f"o{layer}"), start=(layer == CA3), stop=True, skip_group_check=True)
                    last.then_inc(full(item), 1)
                elif kind == "nT":
                    chained(pe, ("norm", item[1], item[2]))
                    turn(item, nrm[UNITS[item[1]][1]])
                elif kind == "xT":
                    taken(pe, ("ssm", item[1]))
                    turn(item, X[item[1]])
                elif kind == "cT":
                    pe.wait_ge(cn_done, CNORMS.index(item[1]) + 1)
                    dst = claim(pe, item)
                    for kt in range(4):
                        last = nc.tensor.transpose(dst[:, kt * 128:(kt + 1) * 128], cn[:, kt, :], id_sb[:, :])
                    last.then_inc(full(item), 1)
                elif kind in ("qproj", "kproj"):
                    u = item[1]
                    layer, b = UNITS[u]
                    if kind == "qproj":
                        source_ready(pe, u)
                        src = query_source(u)
                    else:
                        src = key_source(pe, u)
                    loaded(pe, layer)
                    dst = claim(pe, item)
                    nc.tensor.matmul(dst[:, 0:src.shape[1]], W(f"{kind[0]}{layer}"), src, start=True, stop=True).then_inc(full(item), 1)
                elif kind == "vproj":
                    u = item[1]
                    layer = UNITS[u][0]
                    src = key_source(pe, u)
                    loaded(pe, layer)
                    dst = claim(pe, item)
                    if layer != CA3:
                        bias_rows(dst, f"bv{layer}", KEYS[layer] // 128)
                    for kt in range(KEYS[layer] // 128):
                        to = dst[:, kt * 128:(kt + 1) * 128]
                        last = nc.tensor.matmul(to, src[:, kt * 128:(kt + 1) * 128], W(f"v{layer}"), start=(layer == CA3), stop=True, skip_group_check=True)
                    last.then_inc(full(item), 1)
                elif kind == "glu":
                    u, f = item[1], item[2]
                    b = UNITS[u][1]
                    taken(pe, ("nT", u, "a"))
                    loaded(pe, CA1)
                    dst = claim(pe, item)
                    for i in range(2):
                        at = i * F_FF + f * 128
                        last = nc.tensor.matmul(dst[:, i * T:(i + 1) * T], W("w12")[:, at:at + 128], XT[b][:, :], start=True, stop=True)
                    last.then_inc(full(item), 1)
                elif kind == "relu":
                    u = item[1]
                    taken(pe, ("nT", u, "a"))
                    dst = claim(pe, item)
                    nc.tensor.matmul(dst[:, 0:T], W("f1"), XT[UNITS[u][1]][:, :], start=True, stop=True).then_inc(full(item), 1)
                elif kind == "ffout":
                    u = item[1]
                    layer, b = UNITS[u]
                    glu = layer == CA0
                    dst = claim(pe, item)
                    bias_rows(dst, "b3" if glu else "bf2", QT)
                    for f in range(4 if glu else 1):
                        taken(pe, ("glu", u, f) if glu else ("relu", u))
                        rhs = W("w3")[:, f * 128:(f + 1) * 128] if glu else W("f2")
                        for qt in range(QT):
                            last = nc.tensor.matmul(dst[:, qt * 128:(qt + 1) * 128], hT[:, f, qt * 128:(qt + 1) * 128], rhs, start=False,
                                                    stop=(f == (3 if glu else 0)), skip_group_check=True)
                    last.then_inc(full(item), 1)
                elif kind == "win":
                    u = item[1]
                    taken(pe, ("nT", u, "a"))
                    dst = claim(pe, item)
                    nc.tensor.matmul(dst[:, 0:T], W("win"), XT[UNITS[u][1]][:, :], start=True, stop=True).then_inc(full(item), 1)
                elif kind == "uproj":
                    u = item[1]
                    taken(pe, ("win", u))
                    dst = claim(pe, item)
                    nc.tensor.matmul(dst[0:S_STATE, 0:T], W("bmat"), hT[:, 0, :], start=True, stop=True).then_inc(full(item), 1)
                elif kind == "warm":
                    pe.wait_ge(exp_done, last_step(2 * CA1 + 1))
                    keep_clock(WARM_UP[item[1]])
                elif kind == "scan":
                    scan()
                elif kind == "ssm":
                    b = item[1]
                    pe.wait_ge(states_done, 1)
                    dst = claim(pe, item)
                    for qt in range(QT):
                        to = dst[:, qt * 128:(qt + 1) * 128]
                        nc.tensor.matmul(to, ones_row[:, :], modrow[:, b, :], start=True, stop=False)
                        last = nc.tensor.matmul(to, G[:, qt * 128:(qt + 1) * 128, b], W("cmat", S_STATE), start=False, stop=True)
                    last.then_inc(full(item), 1)
                elif kind == "mod1":
                    loaded(pe, CA1)
                    dst = claim(pe, item)
                    for b in range(B):
                        for kt in range(4):
                            last = nc.tensor.matmul(dst[0:P_PROG, b:b + 1], probs_sb[:, b, kt, :], inv_col[:, :], start=(kt == 0), stop=(kt == 3))
                    last.then_inc(full(item), 1)
                elif kind == "mod2":
                    taken(pe, ("mod1",))
                    dst = claim(pe, item)
                    for b in range(B):
                        to = dst[0:1, b * 128:(b + 1) * 128]
                        nc.tensor.matmul(to, ones_row[:, 0:1], row_sb[:, ROW["bprog"], :], start=True, stop=False)
                        last = nc.tensor.matmul(to, pmean[:, b:b + 1], W("prog", P_PROG), start=False, stop=True)
                    last.then_inc(full(item), 1)
                elif kind == "flag":
                    pe.wait_ge(mask_done, 2)
                    dst = claim(pe, item)
                    nc.tensor.matmul(dst[:, 0:B], ones_row[:, :], flag_row[:, :], start=True, stop=True).then_inc(full(item), 1)

        @block.scalar
        def _(act):
            act.wait_ge(in_first, 64)
            nc.scalar.activation(half_b[:, :], col_sb[:, COL["b12_0"]:COL["b12_0"] + 4], ACT.Copy, scale=0.5).then_inc(half_set, 1)

            for item in SCHED:
                kind = item[0]
                if kind == "step":
                    n = item[1]
                    act.wait_ge(st_full, n + 1)
                    if n >= 3:
                        act.wait_ge(values_done, n - 2)
                    nc.scalar.activation(probs_e[n % 3][:, :], st_ps[n % 2][:, :], ACT.Exp).then_inc(exp_done, 1)
                elif kind == "drain":
                    gi = item[1]
                    act.wait_ge(values_done, STEP_AT[(gi, KEYS[UNITS[GROUPS[gi][0]][0]] // 128 - 1)] + 1)
                    if gi >= 2:
                        filled(act, ("finish", gi - 2))
                    nc.scalar.activation(o_sb[gi % 2][:, :], o_ps[:, 0:T], ACT.Copy).then_inc(o_taken, 1)
                elif kind == "shift":
                    gi = item[1]
                    src = filled(act, item)
                    if gi >= 4:
                        act.wait_ge(shift_landed[gi % 4], 16 * (gi // 4))
                    nc.scalar.activation(shift_t[gi % 4][:, :], src[0:8, 0:T // 2].bitcast(BF16), ACT.Copy).then_inc(free(item), 1)
                elif kind == "attnT":
                    src = filled(act, item)
                    nc.scalar.activation(attnT[UNITS[item[1]][1]][:, :], src[:, 0:T], ACT.Copy).then_inc(free(item), 1)
                elif kind == "nT":
                    u, tag = item[1], item[2]
                    layer, b = UNITS[u]
                    g, bias = NORM_COLS[(layer, tag)]
                    src = filled(act, item)
                    nc.scalar.activation(XT[b][:, :], src[:, 0:T], ACT.Identity, scale=C(g), bias=C(bias) if bias else 0.0).then_inc(free(item), 1)
                elif kind == "xT":
                    src = filled(act, item)
                    nc.scalar.activation(XT[item[1]][:, :], src[:, 0:T], ACT.Copy).then_inc(free(item), 1)
                elif kind == "cT":
                    u = item[1]
                    layer, b = UNITS[u]
                    src = filled(act, item)
                    nc.scalar.activation(cT[:, :], src[:, :], ACT.Identity, scale=C("g_x1" if layer == CA1 else "g_c"),
                                         bias=C("b_x1") if layer == CA1 else 0.0).then_inc(free(item), 1)
                elif kind == "kproj":
                    u = item[1]
                    layer = UNITS[u][0]
                    n, i = KEYS[layer], KSPLITS.index(u)
                    src = filled(act, item)
                    if i >= 1:
                        act.wait_ge(keys_split, i)
                    if layer not in (SA0, SA2):
                        keys_free(act, i)
                        nc.scalar.activation(kp[i % 2][:, 0, 0:n], src[:, 0:n], ACT.Identity, bias=C(f"bk{layer}") if layer != CA3 else 0.0)
                    nc.scalar.activation(kf[:, 0:n], src[:, 0:n], ACT.Identity, bias=C(f"bk{layer}") if layer != CA3 else 0.0)\
                        .then_inc(free(item), 1)
                elif kind == "krest":
                    u = item[1]
                    n, i = KEYS[UNITS[u][0]], KSPLITS.index(u)
                    act.wait_ge(keys_rest, KRESTS.index(u) + 1)
                    nc.scalar.activation(kp[i % 2][:, 1, 0:n], kf[:, 0:n], ACT.Copy).then_inc(keys_second, 1)
                elif kind == "vproj":
                    u = item[1]
                    layer, b = UNITS[u]
                    hd, nkt = head_dim(u), KEYS[layer] // 128
                    src = filled(act, item)
                    if u < 6:
                        act.wait_ge(values_cleared, u + 1)
                    if layer >= SA2:
                        act.wait_ge(values_done, last_step({SA2: 2 * SA0, CA2: 2 * CA0, CA3: 2 * CA1}[layer] + b))
                    if layer == CA3:
                        act.wait_ge(late_cleared, 4)
                        taken(act, ("flag",))
                    nc.scalar.activation(v_pack(u)[:, :, :, 0:hd], src[:, 0:nkt * 128].rearrange("p (t h d) -> p t h d", t=nkt, d=hd),
                                         ACT.Copy, scale=flag[:, b:b + 1] if layer == CA3 else 1.0).then_inc(free(item), 1)
                elif kind == "glu":
                    u, f = item[1], item[2]
                    b = UNITS[u][1]
                    src = filled(act, item)
                    if f >= 2:
                        taken(act, ("glu", u, f - 2))
                    act.wait_ge(half_set, 1)
                    nc.scalar.activation(glu_t[b][f % 2][:, :], src[:, 0:T], ACT.Tanh, scale=0.5, bias=half_b[:, f:f + 1]).then_inc(gate_done, 1)
                elif kind == "relu":
                    src = filled(act, item)
                    nc.scalar.activation(hT[:, 0, :], src[:, 0:T], ACT.Relu, bias=C("b_f1")).then_inc(free(item), 1)
                elif kind == "win":
                    src = filled(act, item)
                    nc.scalar.activation(hT[:, 0, :], src[:, 0:T], ACT.Identity, bias=C("b_in")).then_inc(free(item), 1)
                elif kind == "uproj":
                    src = filled(act, item)
                    nc.scalar.activation(UT[:, :, UNITS[item[1]][1]], src[0:S_STATE, 0:T], ACT.Copy).then_inc(free(item), 1)
                elif kind == "scan":
                    act.wait_ge(scan_pre, 1)
                    for t in range(1, T):
                        if t >= 2:
                            act.wait_ge(scan_h, t - 1)
                        nc.scalar.activation(G[:, t, :], scan_ps[:, (t - 1) * B:t * B], ACT.Silu).then_inc(scan_g, 1)
                elif kind == "mod1":
                    src = filled(act, item)
                    nc.scalar.activation(pmean[:, :], src[0:P_PROG, 0:B], ACT.Copy).then_inc(free(item), 1)
                elif kind == "mod2":
                    src = filled(act, item)
                    nc.scalar.activation(modrow[:, :, :], src[0:1, 0:B * 128].rearrange("p (b d) -> p b d", b=B), ACT.Copy).then_inc(free(item), 1)
                elif kind == "flag":
                    src = filled(act, item)
                    nc.scalar.activation(flag[:, :], src[:, 0:B], ACT.Copy).then_inc(free(item), 1)

        @block.vector
        def _(dve):
            steps = [0]

            def own(ins):
                steps[0] += 1
                ins.then_inc(dve_step, 1)

            def after_own():
                dve.wait_ge(dve_step, steps[0])

            nc.vector.memset(ones_row[:, :], 1.0)
            nc.vector.memset(inv_col[:, :], 1.0 / S2)
            nc.vector.memset(o_ps[:, :], 0.0).then_inc(consts_set, 1)
            own(nc.vector.memset(den_sb[:, :], 0.0))
            after_own()
            nc.vector.memset(den_sb[:, 8:9], 1.0).then_inc(consts_set, 1)

            def residual(u):
                b = UNITS[u][1]
                done = [SIDE[i] for i in SCHED[:SCHED.index(("oproj", u) if ("oproj", u) in BANK else ("zadd", u))] if i[0] == "tok" and UNITS[i[1]][1] == b]
                if done:
                    dve.wait_ge(side_s[b], max(done))
                else:
                    dve.wait_ge(in_next, 64)

            for item in SCHED:
                kind = item[0]
                if kind == "scores":
                    gi, i = item[1], item[2]
                    qt, j0, n = tiles(gi)[i]
                    src = filled(dve, item)
                    nc.vector.tensor_reduce(rowmax[gi % 2][:, qt, j0:j0 + n], src[:, :].rearrange("p (h k) -> p h k", h=n), AX_X, ALU.max)\
                        .then_inc(free(item), 1)
                    if i == len(tiles(gi)) - 1:
                        for t in range(max(0, i - RING + 1), i + 1):
                            taken(dve, ("scores", gi, t))
                        if gi >= 2:
                            filled(dve, ("shift", gi - 2))
                        own(nc.vector.tensor_scalar(shift_p[gi % 2][:, :, 0, :], rowmax[gi % 2][:, :, :], -1.0, None, ALU.mult))
                        after_own()
                        nc.vector.scalar_tensor_tensor(shift_p[gi % 2][:, :, 1, :], rowmax[gi % 2][:, :, :], -1.0,
                                                       shift_p[gi % 2][:, :, 0, :], ALU.mult, ALU.subtract).then_inc(shift_ready, 1)
                elif kind == "idb":
                    dve.wait_ge(in_ident, 16)
                    nc.vector.tensor_copy(idb_sb[:, :], id_sb[:, :]).then_inc(idb_done, 1)
                elif kind == "finish":
                    gi = item[1]
                    u, g = GROUPS[gi]
                    b, hd = UNITS[u][1], head_dim(u)
                    src = filled(dve, item)[:, 0:T].rearrange("p (t j c) -> p t j c", t=QT, j=4)
                    if gi:
                        taken(dve, ("finish", gi - 1))
                    own(nc.vector.reciprocal(rden[:, :, :, :], src[:, :, :, hd:hd + 1]))
                    after_own()
                    for qt in range(QT):
                        last = nc.vector.tensor_tensor(attn[b][:, qt, 4 * g * hd:4 * (g + 1) * hd].rearrange("p (j d) -> p j d", j=4),
                                                       src[:, qt, :, 0:hd], rden[:, qt, :, :].broadcast_to([128, 4, hd]), ALU.mult)
                    last.then_inc(free(item), 1)
                elif kind in ("oproj", "ffout"):
                    u = item[1]
                    layer, b = UNITS[u]
                    src = filled(dve, item)
                    if kind == "ffout":
                        dve.wait_ge(side_s[b], SIDE[("tok", u, "a")])
                    else:
                        residual(u)
                    to = X[b] if layer == CA1 else r[b]
                    nc.vector.tensor_tensor(to[:, :, :], src[:, 0:T].rearrange("p (t d) -> p t d", t=QT), X[b][:, :, :], ALU.add).then_inc(free(item), 1)
                elif kind == "zadd":
                    u = item[1]
                    b = UNITS[u][1]
                    residual(u)
                    dve.wait_ge(z_landed[u], 16)
                    nc.vector.tensor_tensor(r[b][:, :, :], z[b][:, :, :], X[b][:, :, :], ALU.add).then_inc(chain_s[b], 1)
                elif kind == "ssm":
                    b = item[1]
                    src = filled(dve, item)
                    nc.vector.tensor_tensor(X[b][:, :, :], src[:, 0:T].rearrange("p (t d) -> p t d", t=QT), X[b][:, :, :], ALU.add).then_inc(free(item), 1)
                elif kind == "stats":
                    u, tag = item[1], item[2]
                    layer, b = UNITS[u]
                    rms, src = (layer, tag) in RMS, X[b] if (layer, tag) in FROM_X else r[b]
                    if tag == "c":
                        chained(dve, ("tokd", u, "b"))
                    elif tag == "b":
                        taken(dve, ("ffout", u))
                    elif layer in (SA2, CA2):
                        chained(dve, ("zadd", u))
                    else:
                        taken(dve, ("oproj", u))
                    for qt in range(QT):
                        own(nc.vector.bn_stats(stats[b][:, qt, :], src[:, qt, :]))
                    of_stats = steps[0] - QT
                    for qt in range(QT):
                        dve.wait_ge(dve_step, of_stats + qt + 1)
                        own(nc.vector.bn_aggr(mv[b][:, qt, :], stats[b][:, qt, :]))
                    after_own()
                    if rms:
                        own(nc.vector.tensor_tensor(ve[b][:, :], mv[b][:, :, 0], mv[b][:, :, 0], ALU.mult))
                        after_own()
                        nc.vector.scalar_tensor_tensor(ve[b][:, :], mv[b][:, :, 1], EPS[True], ve[b][:, :], ALU.add, ALU.add).then_inc(chain_s[b], 1)
                    else:
                        nc.vector.tensor_scalar(ve[b][:, :], mv[b][:, :, 1], EPS[False], None, ALU.add).then_inc(chain_s[b], 1)
                elif kind == "norm":
                    u, tag = item[1], item[2]
                    layer, b = UNITS[u]
                    rms, src = (layer, tag) in RMS, X[b] if (layer, tag) in FROM_X else r[b]
                    chained(dve, ("pow", u, tag))
                    for qt in range(QT):
                        if rms:
                            last = nc.vector.tensor_scalar(nrm[b][:, qt, :], src[:, qt, :], rs[b][:, qt:qt + 1], None, ALU.mult)
                        else:
                            last = nc.vector.tensor_scalar(nrm[b][:, qt, :], src[:, qt, :], mv[b][:, qt, 0:1], rs[b][:, qt:qt + 1], ALU.subtract, ALU.mult)
                    last.then_inc(chain_s[b], 1)
                elif kind == "tokd":
                    u, tag = item[1], item[2]
                    layer, b = UNITS[u]
                    g, bias = NORM_TOKS[(layer, tag)]
                    chained(dve, ("norm", u, tag))
                    own(nc.vector.tensor_tensor(r[b][:, :, :], nrm[b][:, :, :], tok_sb[:, TOK[g]:TOK[g] + 1, :].broadcast_to([128, QT, D]), ALU.mult))
                    after_own()
                    nc.vector.tensor_tensor(X[b][:, :, :], r[b][:, :, :], tok_sb[:, TOK[bias]:TOK[bias] + 1, :].broadcast_to([128, QT, D]), ALU.add)\
                        .then_inc(chain_s[b], 1)
                elif kind == "outmul":
                    u = item[1]
                    b = UNITS[u][1]
                    chained(dve, ("norm", u, "a"))
                    nc.vector.tensor_tensor(nrm[b][:, :, :], nrm[b][:, :, :], tok_sb[:, TOK["g_out"]:TOK["g_out"] + 1, :].broadcast_to([128, QT, D]), ALU.mult)\
                        .then_inc(chain_s[b], 1)
                elif kind == "qproj":
                    u = item[1]
                    layer, b = UNITS[u]
                    dve.wait_ge(in_first, 64)
                    if u >= 2:
                        dve.wait_ge(q_landed[u - 2], 16 * (TERMS + (UNITS[u - 2][0] == SA2)))
                    src = filled(dve, item)
                    bias = C(f"bq{layer}") if layer != CA3 else 0.0
                    nc.vector.tensor_scalar(qp[b][:, 0, :], src[:, 0:T], bias, SCALE[layer], ALU.add, ALU.mult).then_inc(q_parts[b], 1)
                    nc.vector.tensor_scalar(qf[b][:, :], src[:, 0:T], bias, SCALE[layer], ALU.add, ALU.mult).then_inc(free(item), 1)
                elif kind == "qsplit":
                    u = item[1]
                    b = UNITS[u][1]
                    taken(dve, ("qproj", u))
                    at = PARTS * UNITS[u][0]
                    dve.wait_ge(q_parts[b], at + 1)
                    own(nc.vector.tensor_tensor(qr[b][:, :], qf[b][:, :], qp[b][:, 0, :], ALU.subtract))
                    after_own()
                    nc.vector.tensor_copy(qp[b][:, 1, :], qr[b][:, :]).then_inc(q_parts[b], 1)
                    dve.wait_ge(q_parts[b], at + 2)
                    nc.vector.tensor_tensor(qp[b][:, 2, :], qr[b][:, :], qp[b][:, 1, :], ALU.subtract).then_inc(q_parts[b], 1)
                elif kind == "ksplit" and UNITS[item[1]][0] in (SA0, SA2):
                    u = item[1]
                    n, i = KEYS[UNITS[u][0]], KSPLITS.index(u)
                    p = kp[i % 2]
                    taken(dve, ("kproj", u))
                    keys_free(dve, i)
                    own(nc.vector.tensor_copy(p[:, 0, 0:n], kf[:, 0:n]))
                    after_own()
                    own(nc.vector.tensor_tensor(kf[:, 0:n], kf[:, 0:n], p[:, 0, 0:n], ALU.subtract))
                    after_own()
                    own(nc.vector.tensor_copy(p[:, 1, 0:n], kf[:, 0:n]))
                    after_own()
                    nc.vector.tensor_tensor(p[:, 2, 0:n], kf[:, 0:n], p[:, 1, 0:n], ALU.subtract).then_inc(keys_split, 1)
                elif kind == "glu":
                    u, f = item[1], item[2]
                    b = UNITS[u][1]
                    dve.wait_ge(gate_done, GLUS.index(item) + 1)
                    src = filled(dve, item)
                    own(nc.vector.tensor_scalar(glu_a[b][:, :], src[:, 0:T], C(f"b12_{f}"), 0.5, ALU.add, ALU.mult))
                    after_own()
                    own(nc.vector.scalar_tensor_tensor(glu_w[b][:, :], glu_t[b][f % 2][:, :], 1.0, glu_a[b][:, :], ALU.add, ALU.mult))
                    after_own()
                    nc.vector.scalar_tensor_tensor(hT[:, f, :], src[:, T:2 * T], C(f"b12_{f + 4}"), glu_w[b][:, :], ALU.add, ALU.mult).then_inc(free(item), 1)
                elif kind == "ctxstats":
                    loaded(dve, CA1)
                    for i in range(8):
                        own(nc.vector.bn_stats(cstats[:, i, :], ctx_sb[:, i // 4, i % 4, :]))
                    after_own()
                    for i in range(8):
                        own(nc.vector.bn_aggr(cmv[:, i, :], cstats[:, i, :]))
                    after_own()
                    own(nc.vector.tensor_tensor(cve[:, 1, :], cmv[:, :, 0], cmv[:, :, 0], ALU.mult))
                    after_own()
                    own(nc.vector.scalar_tensor_tensor(cve[:, 1, :], cmv[:, :, 1], EPS[True], cve[:, 1, :], ALU.add, ALU.add))
                    after_own()
                    nc.vector.tensor_scalar(cve[:, 0, :], cmv[:, :, 1], EPS[False], None, ALU.add).then_inc(cstats_done, 1)
                elif kind == "maskprep":
                    own(nc.vector.tensor_scalar(mrow, mask_sb[:, :, :], -1.0, BIG, ALU.add, ALU.mult))
                    after_own()
                    nc.vector.tensor_reduce(flag_row[:, :], mask_sb[:, :, :], AX_X, ALU.max).then_inc(mask_done, 2)
                elif kind == "scan":
                    for b in range(B):
                        taken(dve, ("uproj", 2 * CA1 + b))
                    own(nc.vector.memset(G[:, 0, :], 0.0))
                    after_own()
                    dve.wait_ge(scan_g, T - 1)
                    nc.vector.tensor_tensor(G[:, :, :], G[:, :, :], UT[:, :, :], ALU.add).then_inc(states_done, 1)

        @block.gpsimd
        def _(pool):
            steps = [0]

            def own(ins):
                steps[0] += 1
                ins.then_inc(pool_step, 1)
                pool.wait_ge(pool_step, steps[0])

            own(nc.gpsimd.memset(half[:, :], -0.5))
            for item in SCHED:
                kind = item[0]
                if kind == "clear":
                    what = item[1]
                    if what == "late":
                        to = [k_odd[0][96:128, 0:8 * S2]]
                    else:
                        b = int(what[1])
                        to = [q_pack[b][lo:hi, :] if what[0] == "q" else k_odd[1][lo:hi, b * 16 * T:(b + 1) * 16 * T] for lo, hi in ((32, 64), (64, 128))]
                    for i, t in enumerate(to):
                        nc.gpsimd.memset(t.bitcast(F32), 0.0).then_inc(cleared, 1)
                        pool.wait_ge(cleared, CLEARED[item] - len(to) + i + 1)
                elif kind == "vclear":
                    u = item[1]
                    v = [v_self, v_even, v_odd][u // 2][u % 2]
                    own(nc.gpsimd.memset(v[:, :], 0.0))
                    nc.gpsimd.memset(v_pack(u)[:, :, :, head_dim(u):head_dim(u) + 1], 1.0).then_inc(values_cleared, 1)
                    pool.wait_ge(values_cleared, u + 1)
                elif kind == "kclear":
                    b = item[1]
                    for i, (lo, hi) in enumerate(((32, 64), (64, 128))):
                        nc.gpsimd.memset(k_even[b][lo:hi, :].bitcast(F32), 0.0).then_inc(keys_cleared, 1)
                        pool.wait_ge(keys_cleared, 2 * b + i + 1)
                elif kind == "pow":
                    u, tag = item[1], item[2]
                    b = UNITS[u][1]
                    chained(pool, ("stats", u, tag))
                    nc.gpsimd.tensor_tensor(rs[b][:, :], ve[b][:, :], half[:, 0:QT], ALU.pow).then_inc(chain_s[b], 1)
                    chained(pool, item)
                elif kind == "tok":
                    u, tag = item[1], item[2]
                    layer, b = UNITS[u]
                    g, bias = NORM_TOKS[(layer, tag)]
                    chained(pool, ("norm", u, tag))
                    own(nc.gpsimd.tensor_tensor(X[b][:, :, :], nrm[b][:, :, :], tok_sb[:, TOK[g]:TOK[g] + 1, :].broadcast_to([128, QT, D]), ALU.mult))
                    nc.gpsimd.tensor_tensor(X[b][:, :, :], X[b][:, :, :], tok_sb[:, TOK[bias]:TOK[bias] + 1, :].broadcast_to([128, QT, D]), ALU.add)\
                        .then_inc(side_s[b], 1)
                    pool.wait_ge(side_s[b], SIDE[item])
                elif kind == "krest":
                    u = item[1]
                    n, i = KEYS[UNITS[u][0]], KSPLITS.index(u)
                    taken(pool, ("kproj", u))
                    nc.gpsimd.tensor_tensor(kf[:, 0:n], kf[:, 0:n], kp[i % 2][:, 0, 0:n], ALU.subtract).then_inc(keys_rest, 1)
                    pool.wait_ge(keys_rest, KRESTS.index(u) + 1)
                elif kind == "ksplit" and UNITS[item[1]][0] not in (SA0, SA2):
                    u = item[1]
                    n, i = KEYS[UNITS[u][0]], KSPLITS.index(u)
                    pool.wait_ge(keys_second, KRESTS.index(u) + 1)
                    nc.gpsimd.tensor_tensor(kp[i % 2][:, 2, 0:n], kf[:, 0:n], kp[i % 2][:, 1, 0:n], ALU.subtract).then_inc(keys_split, 1)
                    pool.wait_ge(keys_split, i + 1)
                elif kind == "triangle":
                    n = item[1]
                    gi, kt = STEPS[n]
                    pool.wait_ge(exp_done, n + 1)
                    if n - 2 in MASKED_AT:
                        pool.wait_ge(values_done, n - 1)
                    src = probs_e[n % 3][:, :].rearrange("p (j t) -> p j t", j=4)[:, :, kt * 128:(kt + 1) * 128]
                    nc.gpsimd.tensor_tensor(probs_m[n % 2][:, :, :], src, tri_sb[:, :].unsqueeze(1).broadcast_to([128, 4, 128]), ALU.mult).then_inc(masked, 1)
                    pool.wait_ge(masked, MASKED_AT[n] + 1)
                elif kind == "ctxstats":
                    pool.wait_ge(cstats_done, 1)
                    for i in range(2):
                        nc.gpsimd.tensor_tensor(crs[:, i, :], cve[:, i, :], half[:, :], ALU.pow).then_inc(crs_done, 1)
                        pool.wait_ge(crs_done, i + 1)
                elif kind == "cnorm":
                    u = item[1]
                    layer, b = UNITS[u]
                    i = CNORMS.index(u)
                    pool.wait_ge(crs_done, 2)
                    if i:
                        k, n = BANK[("cT", CNORMS[i - 1])]
                        pool.wait_ge(bank_full[k], n + 1)
                    for kt in range(4):
                        t = 4 * b + kt
                        if layer == CA1:
                            last = nc.gpsimd.tensor_scalar(cn[:, kt, :], ctx_sb[:, b, kt, :], cmv[:, t, 0:1], crs[:, 0, t:t + 1], ALU.subtract, ALU.mult)
                        else:
                            last = nc.gpsimd.tensor_scalar(cn[:, kt, :], ctx_sb[:, b, kt, :], crs[:, 1, t:t + 1], None, ALU.mult)
                        if kt < 3:
                            own(last)
                    last.then_inc(cn_done, 1)
                    pool.wait_ge(cn_done, i + 1)
                elif kind == "mod1":
                    for b in range(B):
                        pool.wait_ge(values_done, last_step(2 * SA0 + b))
                        nc.gpsimd.memset(v_self[b][:, :].rearrange("p (t h c) -> p t h c", h=16, c=16)[:, :, :, 8:9], 0.0).then_inc(ones_cleared, 1)
                        pool.wait_ge(ones_cleared, b + 1)
                elif kind == "scan":
                    pool.wait_ge(st_full, last_step(2 * CA1 + 1))
                    for b in range(B):
                        own(nc.gpsimd.memset(q_pack[b][32:64, :].bitcast(F32), 0.0))
                        own(nc.gpsimd.memset(q_pack[b][64:96, :].bitcast(F32), 0.0))
                    own(nc.gpsimd.memset(k_odd[1][32:64, :].bitcast(F32), 0.0))
                    nc.gpsimd.memset(k_odd[1][64:96, :].bitcast(F32), 0.0).then_inc(late_cleared, 2)
                    pool.wait_ge(late_cleared, 2)
                    pool.wait_ge(values_done, last_step(2 * CA1 + 1))
                    for b in range(B):
                        own(nc.gpsimd.memset(v_odd[b][:, :], 0.0))
                        own(nc.gpsimd.memset(v_odd[b][:, :].rearrange("p (t h c) -> p t h c", h=16, c=16)[:, :, :, 8:9], 1.0))
                    own(nc.gpsimd.memset(k_odd[0][32:64, :].bitcast(F32), 0.0))
                    nc.gpsimd.memset(k_odd[0][64:128, :].bitcast(F32), 0.0).then_inc(late_cleared, 2)
                    pool.wait_ge(late_cleared, 4)



GLUS = [i for i in SCHED if i[0] == "glu"]
MASKED_AT = {n: i for i, n in enumerate(it[1] for it in SCHED if it[0] == "triangle")}


def kernel(**inputs):
    import ml_dtypes
    import concourse.bacc as bacc
    from concourse.bass_utils import run_bass_kernel_spmd

    a = {k: np.asarray(v) for k, v in inputs.items()}
    L0, L1, L2, L3 = (lambda n, i=i: a[f"L{i}_xattn_{n}"] for i in range(4))
    f32 = np.float32

    def pad(m):
        return np.concatenate([m, np.zeros((128 - m.shape[0], m.shape[1]), m.dtype)], 0) if m.shape[0] < 128 else m

    qkv0, kv1, qkv2 = L0("qkv_w").T, L0("kv_w").T, L1("W_qkv").T
    w = {"q0": qkv0[:, 0:128], "k0": qkv0[:, 128:256], "v0": qkv0[:, 256:384], "o0": L0("self_out_w").T,
         "q1": L0("q_w").T, "k1": kv1[:, 0:128], "v1": kv1[:, 128:256], "o1": L0("cross_out_w").T, "w12": L0("w12").T,
         "w3": L0("w3").T.reshape(4, 128, 128).transpose(1, 0, 2).reshape(128, 512),
         "q2": qkv2[:, 0:128], "k2": qkv2[:, 128:256], "v2": qkv2[:, 256:384], "o2": L1("W_o").T, "win": L1("W_in").T,
         "bmat": L1("Bmat"), "at": L1("A").T, "cmat": L1("Cmat"), "prog": L1("W_prog").T,
         "q3": L2("sa_wq"), "k3": L2("sa_wk"), "v3": L2("sa_wv"), "q4": L2("ca_wq"), "k4": L2("ca_wk"), "v4": L2("ca_wv"),
         "f1": L2("ffn_w1"), "f2": L2("ffn_w2"), "q5": L3("Wq"), "k5": L3("Wk"), "v5": L3("Wv"), "o5": L3("Wo")}
    turn = {f"{n}{layer}": np.arange(D).reshape(HEADS[layer], -1).T.ravel() for n in "qk" for layer in range(6)}
    w = np.concatenate([pad(w[n][:, turn[n]] if n in turn else w[n]) for n in W_COLS], 1)
    b0, b2 = L0("qkv_b"), L1("b_qkv")
    col = {"bq0": b0[0:128], "bk0": b0[128:256], "bq1": L0("q_b"), "bk1": L0("kv_b")[0:128], "bq2": b2[0:128], "bk2": b2[128:256],
           "bq3": L2("sa_bq"), "bk3": L2("sa_bk"), "bq4": L2("ca_bq"), "bk4": L2("ca_bk"),
           "g_ln1": L0("ln1_g"), "b_ln1": L0("ln1_b"), "g_ln2": L0("ln2_g"), "b_ln2": L0("ln2_b"),
           "g_x1": L1("g1"), "b_x1": L1("beta1"), "g_x2": L1("g2"), "b_x2": L1("beta2"), "b_in": L1("b_in"),
           "g_sa": L2("sa_g"), "b_sa": L2("sa_b"), "g_ca": L2("ca_g"), "b_ca": L2("ca_b"), "b_f1": L2("ffn_b1"),
           "g_q": L3("g_q"), "g_c": L3("g_c")}
    col |= {f"b12_{i}": L0("b12")[i * 128:(i + 1) * 128] for i in range(8)}
    cols = np.stack([col[n][turn[n[1:]]] if n[1:] in turn else col[n] for n in COLS], 1)
    row = {"bv0": b0[256:384], "bo0": L0("self_out_b"), "bv1": L0("kv_b")[128:256], "bo1": L0("cross_out_b"), "b3": L0("b3"),
           "bv2": b2[256:384], "bo2": L1("b_o"), "bprog": L1("b_prog"), "bv3": L2("sa_bv"), "bv4": L2("ca_bv"), "bf2": L2("ffn_b2")}
    rows = np.stack([row[n] for n in ROWS], 0)[None]
    tok = {"g_ln1": L0("ln1_g"), "b_ln1": L0("ln1_b"), "g_ln2": L0("ln2_g"), "b_ln2": L0("ln2_b"), "g_ln3": L0("ln3_g"), "b_ln3": L0("ln3_b"),
           "g_sa": L2("sa_g"), "b_sa": L2("sa_b"), "g_ca": L2("ca_g"), "b_ca": L2("ca_b"), "g_ffn": L2("ffn_g"), "b_ffn": L2("ffn_b"),
           "g_out": L3("g_out")}
    toks = np.broadcast_to(np.stack([tok[n] for n in TOKS], 0)[None], (128, len(TOKS), 128))
    x, ctx = a["x"], a["ctx_1024"]
    i = np.arange(128)
    dist = -np.abs(np.arange(T)[:, None] - np.arange(T)[None, :]).reshape(2, 128, T).transpose(1, 0, 2)
    slopes = np.stack([np.eye(128) * p for _, p in SLOPE_PARTS], 1)
    arrays = {
        "in_x_tok": x.reshape(B, QT, 128, D).transpose(0, 2, 1, 3),
        "in_x_t": x.transpose(2, 0, 1),
        "in_ctx_tok": ctx.reshape(B, 4, 128, D).transpose(2, 0, 1, 3),
        "in_ctx_t": ctx.transpose(2, 0, 1),
        "in_probs": a["ctxb_2048x64"].reshape(B, 4, 128, P_PROG).transpose(2, 0, 1, 3),
        "in_mask": a["mask_BxS2_bf1"].reshape(1, B, S2).view(np.uint8),
        "in_w": w, "in_cols": cols, "in_rows": rows, "in_toks": toks,
        "in_ident": np.eye(128, dtype=f32),
        "in_dist": dist.astype(ml_dtypes.bfloat16),
        "in_slopes": slopes.astype(ml_dtypes.bfloat16),
        "in_tri": (i[:, None] >= i[None, :]).astype(f32),
        "in_ones": np.ones((2, 16 * S2), ml_dtypes.bfloat16),
    }
    arrays = {k: np.ascontiguousarray(v) for k, v in arrays.items()}
    nc = bacc.Bacc("TRN2", target_bir_lowering=False, num_devices=1)
    args = [nc.dram_tensor(k, v.shape, mybir.dt.from_np(v.dtype), kind="ExternalInput").ap() for k, v in arrays.items()]
    out = nc.dram_tensor("out_dram", (B, T, D), F32, kind="ExternalOutput").ap()
    build_program(nc, *args, out)
    res = run_bass_kernel_spmd(nc, [arrays], core_ids=[0])
    return res.results[0]["out_dram"]
```
